# Optimizing a Trainium2 kernel written in Bass

```python
import numpy as np
import jax
import jax.numpy as jnp

def _softmax(x, axis=-1):
    return jax.nn.softmax(x, axis=axis)

def _gelu(x):
    return jax.nn.gelu(x, approximate=True)

def _silu(x):
    return jax.nn.silu(x)

def _sigmoid(x):
    return jax.nn.sigmoid(x)

def _layernorm(x, axis=-1, eps=1e-05):
    m = jnp.mean(x, axis=axis, keepdims=True)
    v = jnp.var(x, axis=axis, keepdims=True)
    return (x - m) / jnp.sqrt(v + eps)

def _scatter_add(tgt, idx, src, axis=0):
    return tgt.at[idx].add(src)

def _segment_sum(src, seg, n):
    return jax.ops.segment_sum(src, seg, n)
kernel_name = 'mk_seq_preln_d1_jaxref_r8_f7ae14'

def setup_inputs(seed: int=0):
    np.random.seed(seed)
    _w = jnp.asarray

    def _L0_attn_setup():
        import jax, jax.numpy as jnp
        import numpy as np
        DIM = 128
        HEADS = 16
        NEG = 10000000000.0

        def split_heads(v, heads):
            b, s, d = v.shape
            hd = d // heads
            v = v.reshape(b, s, hd, heads)
            return jnp.transpose(v, (0, 3, 1, 2))

        def merge_heads(v):
            b, h, s, hd = v.shape
            v = jnp.transpose(v, (0, 2, 3, 1))
            return v.reshape(b, s, h * hd)
        key = jax.random.key(seed)
        kx, kq, kk, kv, ko = jax.random.split(key, 5)
        x = jax.random.normal(kx, (2, 256, DIM), dtype=jnp.float32)
        qw = 0.05 * jax.random.normal(kq, (DIM, DIM), dtype=jnp.float32)
        kw = 0.05 * jax.random.normal(kk, (DIM, DIM), dtype=jnp.float32)
        vw = 0.05 * jax.random.normal(kv, (DIM, DIM), dtype=jnp.float32)
        ow = 0.05 * jax.random.normal(ko, (DIM, DIM), dtype=jnp.float32)
        return {'x': x, 'qw': qw, 'kw': kw, 'vw': vw, 'ow': ow}
    _L0_attn_in = _L0_attn_setup()

    def _L0_ffn_setup():
        import jax, jax.numpy as jnp
        import numpy as np
        D_MODEL, D_FF, N_EXPERTS, TOP_K = (128, 512, 8, 2)
        B, S = (2, 256)
        key = jax.random.key(seed)
        ks = jax.random.split(key, 7)
        scale = 0.02
        return {'x': jax.random.normal(ks[0], (B, S, D_MODEL), dtype=jnp.float32), 'W1': jax.random.normal(ks[1], (N_EXPERTS, D_MODEL, D_FF), dtype=jnp.float32) * scale, 'b1': jnp.zeros((N_EXPERTS, D_FF), dtype=jnp.float32), 'W2': jax.random.normal(ks[2], (N_EXPERTS, D_FF, D_MODEL), dtype=jnp.float32) * scale, 'b2': jnp.zeros((N_EXPERTS, D_MODEL), dtype=jnp.float32), 'Wg': jax.random.normal(ks[3], (D_MODEL, N_EXPERTS), dtype=jnp.float32) * scale, 'bg': jnp.zeros((N_EXPERTS,), dtype=jnp.float32)}
    _L0_ffn_in = _L0_ffn_setup()
    _d = {'L0_attn_x': _L0_attn_in['x'], 'L0_attn_qw': _L0_attn_in['qw'], 'L0_attn_kw': _L0_attn_in['kw'], 'L0_attn_vw': _L0_attn_in['vw'], 'L0_attn_ow': _L0_attn_in['ow'], 'L0_ffn_W1': _L0_ffn_in['W1'], 'L0_ffn_b1': _L0_ffn_in['b1'], 'L0_ffn_W2': _L0_ffn_in['W2'], 'L0_ffn_b2': _L0_ffn_in['b2'], 'L0_ffn_Wg': _L0_ffn_in['Wg'], 'L0_ffn_bg': _L0_ffn_in['bg']}
    _x0 = _d['L0_attn_x']
    _d['L0_attn_x'] = jax.random.normal(jax.random.fold_in(jax.random.key(seed), 1), (4, 512, 128), dtype=_x0.dtype)
    del _x0
    return _d

def reference(L0_attn_x, L0_attn_qw, L0_attn_kw, L0_attn_vw, L0_attn_ow, L0_ffn_W1, L0_ffn_b1, L0_ffn_W2, L0_ffn_b2, L0_ffn_Wg, L0_ffn_bg):

    def _L0_attn_ref(x, qw, kw, vw, ow):
        import jax, jax.numpy as jnp
        import numpy as np
        DIM = 128
        HEADS = 16
        NEG = 10000000000.0

        def split_heads(v, heads):
            b, s, d = v.shape
            hd = d // heads
            v = v.reshape(b, s, hd, heads)
            return jnp.transpose(v, (0, 3, 1, 2))

        def merge_heads(v):
            b, h, s, hd = v.shape
            v = jnp.transpose(v, (0, 2, 3, 1))
            return v.reshape(b, s, h * hd)
        b, s, d = x.shape
        Q = split_heads(x @ qw, HEADS)
        K = split_heads(x @ kw, HEADS)
        V = split_heads(x @ vw, HEADS)
        score = jnp.einsum('bhqd,bhkd->bhqk', Q, K) / jnp.sqrt(jnp.float32(d))
        causal = jnp.tril(jnp.ones((1, 1, s, s), dtype=score.dtype))
        score = score - NEG * (1.0 - causal)
        weights = jax.nn.softmax(score, axis=-1)
        attn = jnp.einsum('bhqk,bhkd->bhqd', weights, V)
        return merge_heads(attn) @ ow

    def _L0_ffn_ref(x, W1, b1, W2, b2, Wg, bg):
        import jax, jax.numpy as jnp
        import numpy as np
        D_MODEL, D_FF, N_EXPERTS, TOP_K = (128, 512, 8, 2)
        B, S = (2, 256)
        Bx, Sx, d = x.shape
        E = W1.shape[0]
        logits = jnp.einsum('bsd,de->bse', x, Wg) + bg
        topk_scores, topk_idx = jax.lax.top_k(logits, TOP_K)
        topk_scores = jax.nn.softmax(topk_scores, axis=-1)
        tokens = x.reshape(-1, d)
        idx_flat = topk_idx.reshape(-1, TOP_K)
        sc_flat = topk_scores.reshape(-1, TOP_K)
        comb = (jax.nn.one_hot(idx_flat, E, dtype=x.dtype) * sc_flat[..., None]).sum(axis=1)
        h = jnp.einsum('td,edf->etf', tokens, W1) + b1[:, None, :]
        even = (jnp.arange(E) % 2 == 0)[:, None, None]
        a = jnp.where(even, jax.nn.gelu(h, approximate=False), jax.nn.silu(h))
        y = jnp.einsum('etf,efd->etd', a, W2) + b2[:, None, :]
        out = jnp.einsum('te,etd->td', comb, y)
        return out.reshape(Bx, Sx, d)
    x = L0_attn_x
    x = x + _L0_attn_ref(_layernorm(x, axis=-1), L0_attn_qw, L0_attn_kw, L0_attn_vw, L0_attn_ow)
    x = x + _L0_ffn_ref(_layernorm(x, axis=-1), L0_ffn_W1, L0_ffn_b1, L0_ffn_W2, L0_ffn_b2, L0_ffn_Wg, L0_ffn_bg)
    return x

_drawn_inputs = setup_inputs


def setup_inputs(seed=0):
    import zlib

    import numpy as np

    out = dict(_drawn_inputs(seed))
    spreads = {'L0_ffn_b1': (0.0, 0.461), 'L0_ffn_b2': (0.0, 0.1), 'L0_ffn_bg': (0.0, 0.1)}
    factors = {'L0_attn_qw': 8.0, 'L0_attn_kw': 8.0}
    for name, (base, spread) in spreads.items():
        noise = np.random.default_rng([zlib.crc32(name.encode()), seed]).standard_normal(out[name].shape)
        drawn = base * np.exp(spread * noise) if base else spread * noise
        out[name] = jnp.asarray(drawn.astype(out[name].dtype))
    for name, factor in factors.items():
        out[name] = (out[name] * factor).astype(out[name].dtype)
    return out
```

```python
from contextlib import ExitStack

import concourse.bass as bass
from concourse import mybir

F32 = mybir.dt.float32
F32R = mybir.dt.float32r
BF16 = mybir.dt.bfloat16
ALU = mybir.AluOpType
ACT = mybir.ActivationFunctionType
AX_X = mybir.AxisListType.X

P = 128
BATCHES, SEQ = 4, 512
TILES = SEQ // P
HEADS, HD = 16, 8
R = 4
GROUPS = HEADS // R
STEPS = BATCHES * GROUPS
EXPERTS, FF = 8, 512
FT = FF // P
SCALE = float(P) ** -0.5
EPS = 1e-5
MASKED = -1e30
LAG = 3
UNITS = BATCHES * FT

PT_WIDTH = [SEQ - P * j for j in range(TILES)]
PT_AT = [R * sum(PT_WIDTH[:j]) for j in range(TILES)]
PT_SIZE = R * sum(PT_WIDTH)
SHIFTED = [(0, (0, 1)), (0, (2, 3)), (1, (0, 1)), (1, (2, 3)), (2, (0, 1, 2, 3)), (3, (0, 1, 2, 3))]
NSH = len(SHIFTED)
LAST_UNIT = {0: 1, 1: 3, 2: 4, 3: 5}
SCORES = [(r, t) for r in range(R) for t in range(TILES)]
NSC = len(SCORES)
SHIFTED_SLOT = {0: 0, 3: 1, 5: 2, 8: 3, 11: 4, 13: 5}
PV_SLOT = {2: 0, 6: 1, 10: 2, 12: 3}

FIRST_STEP, END_STEP = -4, 4 * (BATCHES - 1) + 8


def batch_at(n, offset):
    b, rest = divmod(n - offset, GROUPS)
    return b if rest == 0 and 0 <= b < BATCHES else None


def plan(n):
    valid = lambda k: 0 <= k < STEPS
    events = []

    def per_batch(name, offset):
        b = batch_at(n, offset)
        if b is not None:
            events.append((name, b, None))

    per_batch("ln2_normalise", 6)
    per_batch("ln1_stats", -4)
    if valid(n + 1):
        events.append(("max_transpose", n + 1, None))
    for slot in range(NSC):
        if valid(n + 2):
            events.append(("scores", n + 2, slot))
        if valid(n) and slot in SHIFTED_SLOT:
            events.append(("shifted", n, SHIFTED_SLOT[slot]))
        if valid(n - 1) and slot in PV_SLOT:
            events.append(("pv", n - 1, PV_SLOT[slot]))
        if slot == 1:
            per_batch("q_project", -3)
            per_batch("x2_transpose", 6)
        if slot == 3:
            per_batch("k_project", -3)
        if slot == 4 and valid(n - 2):
            events.append(("out_transpose", n - 2, None))
        if slot == 6:
            per_batch("ln1_normalise", -4)
        if slot == 8:
            per_batch("attn_transpose", 5)
        if slot == 9:
            per_batch("gate", 6)
        if slot == 13:
            per_batch("gate_finish", 6)
        if slot == 11:
            per_batch("weight_transpose", 7)
        if slot == 14:
            per_batch("v_project", 0)
            per_batch("project", 5)
        if slot == 15:
            per_batch("x_transpose", -4)
    return events


PLAN = [e for n in range(FIRST_STEP, END_STEP) for e in plan(n)]
SHARED = ("max_transpose", "q_project", "k_project", "x2_transpose", "out_transpose", "attn_transpose",
          "gate", "weight_transpose", "v_project", "project", "x_transpose")
SHARED_USE = {(e[0], e[1]): i for i, e in enumerate([e for e in PLAN if e[0] in SHARED])}


def build(nc, x, qw, kw, vw, ow, W1, b1, W2, b2, Wg, bg, out):
    with ExitStack() as ctx:
        def sb(name, shape, dt=F32):
            return ctx.enter_context(nc.sbuf_tensor(name, shape, dt))

        def sem(name):
            return ctx.enter_context(nc.semaphore(name))

        q_planes = nc.dram_tensor("q_planes", (2, HEADS, 4, HD, SEQ), F32, kind="Internal").ap()
        k_planes = nc.dram_tensor("k_planes", (2, HEADS, 4, HD, SEQ), F32, kind="Internal").ap()
        weight_rows = nc.dram_tensor("weight_rows", (BATCHES, EXPERTS, SEQ), F32, kind="Internal").ap()

        ident = sb("ident", [P, P])
        causal = sb("causal", [P, SEQ])
        minus_half = sb("minus_half", [P, TILES])
        rank = sb("rank", [P, EXPERTS])
        plane_const = sb("plane_const", [P, 2, SEQ])
        qw_s, kw_s, vw_s, ow_s = (sb(n, [P, P]) for n in ("qw_s", "kw_s", "vw_s", "ow_s"))
        wg_s = sb("wg_s", [P, EXPERTS])
        bg_s = sb("bg_s", [P, EXPERTS])
        xs = sb("xs", [P, BATCHES, TILES, P])
        stats = sb("stats", [P, TILES, 6])
        moments = sb("moments", [P, TILES, 2])
        var_eps = sb("var_eps", [P, TILES])
        rstd = sb("rstd", [P, TILES])
        xn = sb("xn", [P, TILES, P])
        xn_t = sb("xn_t", [P, SEQ])
        q_hi, q_lo, k_hi, k_lo = (sb(n, [P, SEQ], F32R) for n in ("q_hi", "q_lo", "k_hi", "k_lo"))
        q_stack = sb("q_stack", [P, GROUPS, R, SEQ], F32R)
        k_stack = sb("k_stack", [P, GROUPS, SEQ], F32R)
        v_ones = sb("v_ones", [P, TILES, HEADS, 32])
        row_max = sb("row_max", [P, 2, R * TILES])
        neg_max = sb("neg_max", [R * TILES, 2, P], F32R)
        scratch = sb("scratch", [P, 4, SEQ], BF16)
        p_t = sb("p_t", [P, 2, PT_SIZE])
        pv_s = sb("pv_s", [P, 2, SEQ])
        rsum = sb("rsum", [P, TILES, R])
        attn = sb("attn", [P, TILES, P])
        attn_t = sb("attn_t", [P, SEQ])
        x2n = sb("x2n", [P, TILES, P])
        x2n_t = sb("x2n_t", [P, SEQ])
        x_hi = sb("x_hi", [P, BATCHES, SEQ], F32R)
        x_lo = sb("x_lo", [P, BATCHES, SEQ], F32R)
        gate_f = sb("gate_f", [P, 8, TILES, EXPERTS])
        gate_s = sb("gate_s", [P, 9, TILES])
        weights = sb("weights", [P, EXPERTS, TILES])
        weights_t = sb("weights_t", [EXPERTS * TILES, P])
        w1_in = sb("w1_in", [P, 2, FF])
        w2_in = sb("w2_in", [P, 2, FT, P])
        w1_hi, w1_lo = (sb(n, [P, 2, FF], F32R) for n in ("w1_hi", "w1_lo"))
        w2_hi, w2_lo = (sb(n, [P, 2, FT, P], F32R) for n in ("w2_hi", "w2_lo"))
        b1_s = sb("b1_s", [P, 2, FT])
        b2_s = sb("b2_s", [P, 2])
        y_w = sb("y_w", [P, SEQ])
        acc = sb("acc", [P, BATCHES, SEQ])
        act_f = p_t[:, 0, 0:FT * SEQ].rearrange("p (f t) -> p f t", f=FT)
        weight_bc = p_t[:, 1, 0:2 * BATCHES * SEQ].rearrange("p (e t) -> p e t", e=2)
        act_hi = k_stack
        act_lo = q_stack[:, 0]

        bank_01 = ctx.enter_context(nc.psum_tensor("bank_01", [P, 2, SEQ], F32))
        bank_25 = ctx.enter_context(nc.psum_tensor("bank_25", [P, 4, SEQ], F32))
        bank_67 = ctx.enter_context(nc.psum_tensor("bank_67", [P, 2, SEQ], F32))
        ps_scores, ps_shifted = bank_01, bank_25
        ps_pv, ps_shared = bank_67[:, 0], bank_67[:, 1]
        ps_y, ps_h, ps_final = bank_01, bank_25, bank_67

        x0_loaded, x_loaded = sem("x0_loaded"), sem("x_loaded")
        w_loaded = sem("w_loaded")
        ident_ready, causal_ready, consts_ready = sem("ident_ready"), sem("causal_ready"), sem("consts_ready")
        stacks_cleared, v_cleared = sem("stacks_cleared"), sem("v_cleared")
        planes_cleared = sem("planes_cleared")
        dve_chain, pool_chain = sem("dve_chain"), sem("pool_chain")
        var_ready, rstd_ready = sem("var_ready"), sem("rstd_ready")
        xn_ready = sem("xn_ready")
        q_hi_ready, k_hi_ready = sem("q_hi_ready"), sem("k_hi_ready")
        planes_written = sem("planes_written")
        stack_loaded = [sem("stack_loaded_even"), sem("stack_loaded_odd")]
        max_loaded = [sem("max_loaded_even"), sem("max_loaded_odd")]
        scores_ready, max_done = sem("scores_ready"), sem("max_done")
        shared_filled, shared_drained = sem("shared_filled"), sem("shared_drained")
        shifted_ready, exp_done, causal_done = sem("shifted_ready"), sem("exp_done"), sem("causal_done")
        pv_done, pv_saved = sem("pv_done"), sem("pv_saved")
        x2n_ready, x2_split = sem("x2n_ready"), sem("x2_split")
        gap_ready, gap_exp = sem("gap_ready"), sem("gap_exp")
        weights_ready, weights_written = sem("weights_ready"), sem("weights_written")
        w12_loaded = [sem("w12_loaded_even"), sem("w12_loaded_odd")]
        aux_loaded = [sem("aux_loaded_even"), sem("aux_loaded_odd")]
        w12_split = sem("w12_split")
        h_ready = sem("h_ready")
        act_done = sem("act_done")
        lo_done = sem("lo_done")
        unit_done = sem("unit_done")
        y_free = sem("y_free")
        acc_done = sem("acc_done")
        final_ready, out_ready, out_stored = sem("final_ready"), sem("out_ready"), sem("out_stored")

        filled = lambda stage, n: SHARED_USE[stage, n] + 1
        drained = filled

        x_tiles = x.rearrange("b (t p) d -> p b t d", p=P)
        out_tiles = out.rearrange("b (t p) d -> p b t d", p=P)
        expert_of = lambda k: 2 * k if k < EXPERTS // 2 else 2 * (k - EXPERTS // 2) + 1

        block = ctx.enter_context(nc.Block())

        @block.sync
        def _(sp):
            sp.dma_start(xs[:, 0], x_tiles[:, 0]).then_inc(x0_loaded, 16)
            for dst, src in ((qw_s, qw), (kw_s, kw), (vw_s, vw), (ow_s, ow), (wg_s, Wg)):
                sp.dma_start(dst[:, :], src).then_inc(w_loaded, 16)
            sp.dma_start(bg_s[:, :], bg.rearrange("(a e) -> a e", a=1).to_broadcast([P, EXPERTS])).then_inc(w_loaded, 16)
            sp.wait_ge(consts_ready, 1)
            for par in range(2):
                for planes, c in ((q_planes, 0), (k_planes, 1)):
                    sp.dma_start(planes[par].rearrange("h c i t -> c h (i t)")[3],
                                 plane_const[:, c]).then_inc(planes_cleared, 16)
            sp.dma_start(xs[:, 1:], x_tiles[:, 1:]).then_inc(x_loaded, 16)

            def load_expert(k):
                e, slot = expert_of(k), k % 2
                if k >= 2:
                    sp.wait_ge(acc_done, 1 + BATCHES * (k - 1))
                sp.dma_start(w1_in[:, slot], W1[e]).then_inc(w12_loaded[slot], 16)
                sp.dma_start(w2_in[:, slot], W2[e].rearrange("(f p) d -> p f d", p=P)).then_inc(w12_loaded[slot], 16)

            def load_expert_aux(k):
                e, slot = expert_of(k), k % 2
                sp.dma_start(b1_s[:, slot], b1[e]).then_inc(aux_loaded[slot], 16)
                sp.dma_start(b2_s[:, slot:slot + 1], b2[e]).then_inc(aux_loaded[slot], 16)
                src = weight_rows[:, e]
                dst = weight_bc[:, slot].rearrange("p (b t) -> p b t", b=BATCHES)
                for b in range(BATCHES):
                    sp.dma_start(dst[:, b], src[b:b + 1].to_broadcast([P, SEQ])).then_inc(aux_loaded[slot], 16)

            def load_stacks(n):
                b, g = divmod(n, GROUPS)
                if n == 0:
                    sp.wait_ge(planes_cleared, 16 * 4)
                if n < GROUPS:
                    sp.wait_ge(stacks_cleared, n + 1)
                if g == 0:
                    sp.wait_ge(planes_written, 16 * 6 * (b + 1))
                if n >= GROUPS:
                    sp.wait_ge(shifted_ready, NSH * (n - GROUPS + 1))
                for r in range(R):
                    sp.dma_start(q_stack[32 * r:32 * r + 32, g, r].bitcast(F32),
                                 q_planes[b % 2][R * g + r].rearrange("c i t -> (c i) t"))\
                        .then_inc(stack_loaded[n % 2], 16)
                sp.dma_start(k_stack[:, g].bitcast(F32),
                             k_planes[b % 2][R * g:R * g + R].rearrange("r c i t -> (r c i) t"))\
                    .then_inc(stack_loaded[n % 2], 16)

            load_expert(0)
            load_expert(1)
            for stage, n, i in PLAN:
                if stage == "max_transpose":
                    sp.wait_ge(shared_drained, drained(stage, n))
                    for r in range(R):
                        row = 32 * r + 3 * HD
                        sp.dma_start(q_stack[row:row + 1, n % GROUPS, r].bitcast(F32),
                                     neg_max[r * TILES:(r + 1) * TILES, n % 2].bitcast(F32))\
                            .then_inc(max_loaded[n % 2], 16)
                if stage == "k_project":
                    b, par = n, n % 2
                    if b >= 2:
                        sp.wait_ge(stack_loaded[0], 16 * (R + 1) * 2 * (b - 1))
                        sp.wait_ge(stack_loaded[1], 16 * (R + 1) * 2 * (b - 1))
                    sp.wait_ge(shared_drained, drained("q_project", b))
                    q_dst = q_planes[par].rearrange("h c i t -> c h (i t)")
                    k_dst = k_planes[par].rearrange("h c i t -> c h (i t)")
                    for dst, src in ((q_dst[0], q_hi), (q_dst[1], q_hi), (q_dst[2], q_lo)):
                        sp.dma_start(dst, src[:, :].bitcast(F32)).then_inc(planes_written, 16)
                    sp.wait_ge(shared_drained, drained("k_project", b))
                    for dst, src in ((k_dst[0], k_hi), (k_dst[1], k_lo), (k_dst[2], k_hi)):
                        sp.dma_start(dst, src[:, :].bitcast(F32)).then_inc(planes_written, 16)
                    if b == 0:
                        load_stacks(0)
                if (stage, i) == ("scores", 5) and n + 1 < STEPS:
                    load_stacks(n + 1)
                if stage == "weight_transpose":
                    sp.wait_ge(shared_drained, drained(stage, n))
                    sp.dma_start(weight_rows[n].rearrange("e (q t) -> (e q) t", q=TILES), weights_t[:, :])\
                        .then_inc(weights_written, 16)
            sp.wait_ge(weights_written, 16 * BATCHES)
            sp.wait_ge(pv_done, STEPS)
            for k in range(EXPERTS):
                if k >= 2:
                    load_expert(k)
                load_expert_aux(k)
            for b in range(BATCHES):
                sp.wait_ge(out_ready, b + 1)
                sp.dma_start(out_tiles[:, b], xs[:, b]).then_inc(out_stored, 16)
            sp.wait_ge(out_stored, 16 * BATCHES)

        @block.tensor
        def _(pe):
            def shared(stage, n):
                if SHARED_USE[stage, n]:
                    pe.wait_ge(shared_drained, SHARED_USE[stage, n])

            pe.wait_ge(ident_ready, 1)
            for stage, n, i in PLAN:
                if stage == "scores":
                    r, t = SCORES[i]
                    unit = NSC * n + i
                    if i == 0:
                        pe.wait_ge(stack_loaded[n % 2], 16 * (R + 1) * (n // 2 + 1))
                    if unit >= 2:
                        pe.wait_ge(max_done, unit - 1)
                    width = max(P * (t + 1), 2 * P)
                    nc.tensor.matmul(ps_scores[:, unit % 2, 0:width],
                                     q_stack[:, n % GROUPS, r, t * P:(t + 1) * P],
                                     k_stack[:, n % GROUPS, 0:width], start=True, stop=True)\
                        .then_inc(scores_ready, 1)
                elif stage == "max_transpose":
                    shared(stage, n)
                    pe.wait_ge(max_done, NSC * (n + 1))
                    nc.tensor.transpose(ps_shared[0:R * TILES, 0:P], row_max[:, n % 2], ident[:, :])\
                        .then_inc(shared_filled, 1)
                elif stage == "shifted":
                    j, heads = SHIFTED[i]
                    unit = NSH * n + i
                    if i == 0:
                        pe.wait_ge(max_loaded[n % 2], 16 * R * (n // 2 + 1))
                    if unit >= 2:
                        pe.wait_ge(exp_done, unit - 1)
                    q0 = min(P * j, SEQ - 2 * P)
                    per_bank = len(heads) // 2
                    for at, r in enumerate(heads):
                        bank, col = 2 * (unit % 2) + at // per_bank, (at % per_bank) * (SEQ - q0)
                        last = nc.tensor.matmul(ps_shifted[:, bank, col:col + SEQ - q0],
                                                k_stack[:, n % GROUPS, j * P:(j + 1) * P],
                                                q_stack[:, n % GROUPS, r, q0:SEQ], start=True, stop=True,
                                                skip_group_check=True)
                    last.then_inc(shifted_ready, 1)
                elif stage == "pv":
                    j = i
                    pe.wait_ge(causal_done, TILES * n + j + 1)
                    if j == 0:
                        pe.wait_ge(shared_drained, drained("v_project", n // GROUPS))
                        if n:
                            pe.wait_ge(pv_saved, n)
                    for r in range(R):
                        at = PT_AT[j] + r * PT_WIDTH[j]
                        last = nc.tensor.matmul(ps_pv[32 * r:32 * r + 32, j * P:SEQ],
                                                v_ones[:, j, R * (n % GROUPS) + r],
                                                p_t[:, n % 2, at:at + PT_WIDTH[j]],
                                                start=(j == 0), stop=(j == TILES - 1), skip_group_check=True)
                    if j == TILES - 1:
                        last.then_inc(pv_done, 1)
                elif stage == "out_transpose":
                    shared(stage, n)
                    pe.wait_ge(pv_saved, n + 1)
                    for t in range(TILES):
                        last = nc.tensor.transpose(ps_shared[:, t * P:(t + 1) * P],
                                                   pv_s[:, n % 2, t * P:(t + 1) * P], ident[:, :])
                    last.then_inc(shared_filled, 1)
                elif stage in ("x_transpose", "attn_transpose", "x2_transpose"):
                    shared(stage, n)
                    ready, count, src = {"x_transpose": (xn_ready, n + 1, xn),
                                         "attn_transpose": (shared_drained, SHARED_USE[stage, n], attn),
                                         "x2_transpose": (x2n_ready, n + 1, x2n)}[stage]
                    pe.wait_ge(ready, count)
                    for t in range(TILES):
                        last = nc.tensor.transpose(ps_shared[:, t * P:(t + 1) * P], src[:, t], ident[:, :])
                    last.then_inc(shared_filled, 1)
                elif stage in ("q_project", "k_project"):
                    shared(stage, n)
                    if n == 0:
                        pe.wait_ge(w_loaded, 16 * 6)
                    w = qw_s if stage == "q_project" else kw_s
                    nc.tensor.matmul(ps_shared, w[:, :], xn_t[:, :], start=True, stop=True)\
                        .then_inc(shared_filled, 1)
                elif stage == "v_project":
                    shared(stage, n)
                    for t in range(TILES):
                        last = nc.tensor.matmul(ps_shared[:, t * P:(t + 1) * P], xn_t[:, t * P:(t + 1) * P],
                                                vw_s[:, :], start=True, stop=True, skip_group_check=True)
                    last.then_inc(shared_filled, 1)
                elif stage == "project":
                    shared(stage, n)
                    for t in range(TILES):
                        last = nc.tensor.matmul(ps_shared[:, t * P:(t + 1) * P], attn_t[:, t * P:(t + 1) * P],
                                                ow_s[:, :], start=True, stop=True, skip_group_check=True)
                    last.then_inc(shared_filled, 1)
                elif stage == "gate":
                    shared(stage, n)
                    for t in range(TILES):
                        last = nc.tensor.matmul(ps_shared[:, t * EXPERTS:(t + 1) * EXPERTS],
                                                x2n_t[:, t * P:(t + 1) * P], wg_s[:, :],
                                                start=True, stop=True, skip_group_check=True)
                    last.then_inc(shared_filled, 1)
                elif stage == "weight_transpose":
                    shared(stage, n)
                    pe.wait_ge(weights_ready, n + 1)
                    nc.tensor.transpose(ps_shared[0:EXPERTS * TILES, 0:P],
                                        weights[:, :, :].rearrange("p e t -> p (e t)"), ident[:, :])\
                        .then_inc(shared_filled, 1)

            def up(local, pair):
                unit = UNITS * 2 * pair + local
                k2, b, f = (local // UNITS) % 2, (local // FT) % BATCHES, local % FT
                if local % UNITS == 0:
                    pe.wait_ge(w12_split, 2 * pair + local // UNITS + 1)
                pe.wait_ge(act_done, 2 * unit + 2)
                cols = slice(f * P, (f + 1) * P)
                for i, (w, xx) in enumerate(((w1_hi, x_hi), (w1_hi, x_lo), (w1_lo, x_hi))):
                    last = nc.tensor.matmul(ps_h[:, f], w[:, k2, cols], xx[:, b], start=(i == 0), stop=(i == 2))
                last.then_inc(h_ready, 1)

            def down(local, pair):
                unit = UNITS * 2 * pair + local
                k2, b, f = local // UNITS, (local // FT) % BATCHES, local % FT
                pe.wait_ge(lo_done, unit + 1)
                if f == 0:
                    pe.wait_ge(y_free, 2 * BATCHES * pair + local // FT + 1)
                for i, (w, aa) in enumerate(((w2_hi, act_hi), (w2_hi, act_lo), (w2_lo, act_hi))):
                    last = nc.tensor.matmul(ps_y[:, (local // FT) % 2], w[:, k2, f], aa[:, f],
                                            start=(f == 0 and i == 0), stop=(f == FT - 1 and i == 2))
                last.then_inc(unit_done, 1)

            pe.wait_ge(x2_split, BATCHES)
            pe.wait_ge(exp_done, NSH * STEPS)
            pe.sem_inc(unit_done, FT)
            for local in range(LAG):
                up(local, 0)
            with pe.Fori(0, EXPERTS // 2 - 1) as pair:
                for local in range(2 * UNITS):
                    down(local, pair)
                    up(local + LAG, pair)
            for local in range(2 * UNITS):
                down(local, EXPERTS // 2 - 1)
                if local + LAG < 2 * UNITS:
                    up(local + LAG, EXPERTS // 2 - 1)
            for b in range(BATCHES):
                pe.wait_ge(acc_done, 1 + (EXPERTS - 1) * BATCHES + b + 1)
                if b >= 2:
                    pe.wait_ge(out_ready, b - 1)
                for t in range(TILES):
                    last = nc.tensor.transpose(ps_final[:, b % 2, t * P:(t + 1) * P],
                                               acc[:, b, t * P:(t + 1) * P], ident[:, :])
                last.then_inc(final_ready, 1)

        @block.scalar
        def _(act):
            def from_shared(stage, n, dst, src, signal=shared_drained, scale=1.0):
                act.wait_ge(shared_filled, filled(stage, n))
                nc.scalar.activation(dst, src, ACT.Copy, scale=scale).then_inc(signal, 1)

            for stage, n, i in PLAN:
                if stage == "max_transpose":
                    if n >= 2:
                        act.wait_ge(max_loaded[n % 2], 16 * R * (n // 2))
                    from_shared(stage, n, neg_max[:, n % 2], ps_shared[0:R * TILES, 0:P], scale=-1.0)
                elif stage == "shifted":
                    j, heads = SHIFTED[i]
                    unit = NSH * n + i
                    act.wait_ge(shifted_ready, unit + 1)
                    if i == 0 and n >= 2:
                        act.wait_ge(pv_done, n - 1)
                    width = PT_WIDTH[j]
                    at = PT_AT[j] + heads[0] * width
                    made = max(width, 2 * P)
                    banks = ps_shifted[:, 2 * (unit % 2):2 * (unit % 2) + 2]
                    if j < 2:
                        src = banks[:, :, 0:width]
                    else:
                        src = banks.rearrange("p k (h q) -> p (k h) q", q=made)[:, :, made - width:made]
                    nc.scalar.activation(
                        p_t[:, n % 2, at:at + len(heads) * width].rearrange("p (h q) -> p h q", q=width),
                        src, ACT.Exp, scale=SCALE).then_inc(exp_done, 1)
                elif stage == "pv" and i == TILES - 1:
                    act.wait_ge(pv_done, n + 1)
                    if n >= 2:
                        act.wait_ge(shared_filled, filled("out_transpose", n - 2))
                    nc.scalar.activation(pv_s[:, n % 2], ps_pv, ACT.Copy).then_inc(pv_saved, 1)
                elif stage == "x_transpose":
                    from_shared(stage, n, xn_t[:, :], ps_shared)
                elif stage == "q_project":
                    if n:
                        act.wait_ge(planes_written, 16 * 6 * n)
                    from_shared(stage, n, q_hi[:, :], ps_shared, q_hi_ready)
                elif stage == "k_project":
                    from_shared(stage, n, k_hi[:, :], ps_shared, k_hi_ready)
                elif stage == "v_project":
                    act.wait_ge(v_cleared, 2)
                    from_shared(stage, n, v_ones[:, :, :, 0:HD].rearrange("p t h i -> p t i h"),
                                ps_shared.rearrange("p (t i h) -> p t i h", t=TILES, i=HD))
                elif stage == "attn_transpose":
                    from_shared(stage, n, attn_t[:, :], ps_shared)
                elif stage == "x2_transpose":
                    if n:
                        act.wait_ge(x2_split, n)
                    from_shared(stage, n, x2n_t[:, :], ps_shared)
                elif stage == "gate":
                    act.wait_ge(gap_ready, n + 1)
                    nc.scalar.activation(gate_s[:, 5], gate_s[:, 4], ACT.Exp).then_inc(gap_exp, 1)
                elif stage == "weight_transpose":
                    if n:
                        act.wait_ge(weights_written, 16 * n)
                    from_shared(stage, n, weights_t[:, :], ps_shared[0:EXPERTS * TILES, 0:P])

            act.sem_inc(act_done, 2 * FT)
            for func, first in ((ACT.Gelu, 0), (ACT.Silu, EXPERTS // 4)):
                with act.Fori(first, first + EXPERTS // 4) as pair:
                    for local in range(2 * UNITS):
                        unit = UNITS * 2 * pair + local
                        slot, f = local // UNITS, local % FT
                        if local % UNITS == 0:
                            act.wait_ge(aux_loaded[slot], 16 * (2 + BATCHES) * (pair + 1))
                        act.wait_ge(h_ready, unit + 1)
                        act.wait_ge(unit_done, unit + 1)
                        for dst in (act_f, act_hi):
                            nc.scalar.activation(dst[:, f], ps_h[:, f], func, bias=b1_s[:, slot, f:f + 1])\
                                .then_inc(act_done, 1)

        @block.vector
        def _(dve):
            chain = [0]

            def link(ins):
                chain[0] += 1
                ins.then_inc(dve_chain, 1)
                dve.wait_ge(dve_chain, chain[0])

            nc.vector.memset(plane_const[:, 0], 0.0)
            nc.vector.memset(plane_const[:, 1], 1.0).then_inc(consts_ready, 1)

            def ln_stats(src):
                for t in range(TILES):
                    last = nc.vector.bn_stats(stats[:, t], src[:, t])
                link(last)
                for t in range(TILES):
                    last = nc.vector.bn_aggr(moments[:, t], stats[:, t])
                link(last)
                nc.vector.tensor_scalar(var_eps[:, :], moments[:, :, 1], EPS, None, ALU.add).then_inc(var_ready, 1)

            def ln_normalise(dst, src, ready, count):
                dve.wait_ge(rstd_ready, count)
                for t in range(TILES):
                    last = nc.vector.tensor_scalar(dst[:, t], src[:, t], moments[:, t, 0:1], rstd[:, t:t + 1],
                                                   ALU.subtract, ALU.mult)
                last.then_inc(ready, 1)

            per_expert = lambda s: s.unsqueeze(2).to_broadcast([P, TILES, EXPERTS])
            per_tile = lambda s: s[:, :].unsqueeze(1).to_broadcast([P, TILES, EXPERTS])

            def first_largest(values, top, chosen, equal, ranked, best):
                link(nc.vector.tensor_reduce(top, values, AX_X, ALU.max))
                link(nc.vector.tensor_tensor(equal, values, per_expert(top), ALU.is_equal))
                link(nc.vector.tensor_tensor(ranked, equal, per_tile(rank), ALU.mult))
                link(nc.vector.tensor_reduce(best, ranked, AX_X, ALU.max))
                link(nc.vector.tensor_tensor(chosen, ranked, per_expert(best), ALU.is_equal))

            logits, equal, ranked, first, others, second, part_1, part_2 = (gate_f[:, i] for i in range(8))
            top_1, best, top_2, _, gap, gap_e, total, share_1, share_2 = (gate_s[:, i] for i in range(9))
            normalised = 0
            for stage, n, i in PLAN:
                if stage == "ln1_stats":
                    dve.wait_ge(x_loaded, 16) if n else dve.wait_ge(x0_loaded, 16)
                    ln_stats(xs[:, n])
                elif stage == "ln1_normalise":
                    normalised += 1
                    if n:
                        dve.wait_ge(shared_filled, filled("x_transpose", n - 1))
                    ln_normalise(xn, xs[:, n], xn_ready, normalised)
                elif stage == "ln2_normalise":
                    normalised += 1
                    if n:
                        dve.wait_ge(shared_filled, filled("x2_transpose", n - 1))
                    ln_normalise(x2n, xs[:, n], x2n_ready, normalised)
                elif stage == "scores":
                    r, t = SCORES[i]
                    unit = NSC * n + i
                    if i == 0:
                        dve.wait_ge(causal_ready, 1)
                        if n >= 2:
                            dve.wait_ge(shared_filled, filled("max_transpose", n - 2))
                    dve.wait_ge(scores_ready, unit + 1)
                    if unit >= 4:
                        dve.wait_ge(max_done, unit - 3)
                    width = P * (t + 1)
                    col = r * TILES + t
                    nc.vector.tensor_tensor_reduce(
                        out=scratch[:, unit % 4, 0:width], in0=ps_scores[:, unit % 2, 0:width],
                        in1=causal[:, SEQ - width:SEQ], scale=1.0, scalar=MASKED, op0=ALU.add, op1=ALU.max,
                        accum_out=row_max[:, n % 2, col:col + 1]).then_inc(max_done, 1)
                elif stage in ("q_project", "k_project"):
                    hi, lo, ready = (q_hi, q_lo, q_hi_ready) if stage == "q_project" else (k_hi, k_lo, k_hi_ready)
                    dve.wait_ge(ready, n + 1)
                    nc.vector.tensor_tensor(lo[:, :], ps_shared, hi[:, :].bitcast(F32), ALU.subtract)\
                        .then_inc(shared_drained, 1)
                elif stage == "out_transpose":
                    dve.wait_ge(shared_filled, filled(stage, n))
                    b, g = divmod(n, GROUPS)
                    if g == 0 and b:
                        dve.wait_ge(shared_filled, filled("attn_transpose", b - 1))
                    heads = ps_shared.rearrange("p (t r c) -> p t r c", t=TILES, c=32)
                    link(nc.vector.reciprocal(rsum[:, :, :], heads[:, :, :, HD]))
                    nc.vector.tensor_tensor(
                        attn[:, :, :].rearrange("p t (i g r) -> p t g r i", i=HD, g=GROUPS)[:, :, g],
                        heads[:, :, :, 0:HD], rsum[:, :, :].unsqueeze(3).to_broadcast([P, TILES, R, HD]),
                        ALU.mult).then_inc(shared_drained, 1)
                elif stage == "project":
                    dve.wait_ge(shared_filled, filled(stage, n))
                    flat = xs[:, n].rearrange("p t d -> p (t d)")
                    nc.vector.tensor_tensor(flat, ps_shared, flat, ALU.add).then_inc(shared_drained, 1)
                    dve.wait_ge(shared_drained, drained(stage, n))
                    ln_stats(xs[:, n])
                elif stage == "gate":
                    dve.wait_ge(shared_filled, filled(stage, n))
                    if n:
                        dve.wait_ge(weights_ready, n)
                    else:
                        dve.wait_ge(w_loaded, 16 * 6)
                    nc.vector.tensor_tensor(
                        logits, ps_shared[:, 0:TILES * EXPERTS].rearrange("p (t e) -> p t e", t=TILES),
                        per_tile(bg_s), ALU.add).then_inc(shared_drained, 1)
                    dve.wait_ge(shared_drained, drained(stage, n))
                    first_largest(logits, top_1, first, equal, ranked, best)
                    link(nc.vector.scalar_tensor_tensor(out=others, in0=first, scalar=MASKED, in1=logits,
                                                        op0=ALU.mult, op1=ALU.add))
                    first_largest(others, top_2, second, equal, ranked, best)
                    nc.vector.tensor_tensor(gap, top_2, top_1, ALU.subtract).then_inc(gap_ready, 1)
                elif stage == "gate_finish":
                    dve.wait_ge(gap_exp, n + 1)
                    link(nc.vector.tensor_scalar(total, gap_e, 1.0, None, ALU.add))
                    link(nc.vector.reciprocal(share_1, total))
                    link(nc.vector.tensor_tensor(share_2, gap_e, share_1, ALU.mult))
                    link(nc.vector.tensor_tensor(part_1, first, per_expert(share_1), ALU.mult))
                    link(nc.vector.tensor_tensor(part_2, second, per_expert(share_2), ALU.mult))
                    if n:
                        dve.wait_ge(shared_filled, filled("weight_transpose", n - 1))
                    nc.vector.tensor_tensor(weights[:, :, :].rearrange("p e t -> p t e"), part_1, part_2, ALU.add)\
                        .then_inc(weights_ready, 1)

            def split_lo(local, pair):
                f = local % FT
                dve.wait_ge(act_done, 2 * (2 * UNITS * pair + local + 1) + 2 * FT)
                nc.vector.tensor_tensor(act_lo[:, f], act_f[:, f], act_hi[:, f].bitcast(F32), ALU.subtract)\
                    .then_inc(lo_done, 1)

            def add_expert(q, pair):
                slot, b = q // BATCHES, q % BATCHES
                done = 2 * BATCHES * pair + q
                if q % BATCHES == 0:
                    dve.wait_ge(aux_loaded[slot], 16 * (2 + BATCHES) * (pair + 1))
                dve.wait_ge(unit_done, FT * (done + 1) + FT)
                dve.wait_ge(acc_done, done + 1)
                nc.vector.scalar_tensor_tensor(
                    out=y_w[:, :], in0=ps_y[:, q % 2], scalar=b2_s[:, slot:slot + 1],
                    in1=weight_bc[:, slot, b * SEQ:(b + 1) * SEQ], op0=ALU.add, op1=ALU.mult).then_inc(y_free, 1)
                dve.wait_ge(y_free, done + 1 + 2)
                nc.vector.tensor_tensor(acc[:, b], acc[:, b], y_w[:, :], ALU.add).then_inc(acc_done, 1)

            def expert_pair(pair, last):
                for q in range(2 * BATCHES):
                    for local in range(FT * q + 1, FT * (q + 1) + 1):
                        if not (last and local == 2 * UNITS):
                            split_lo(local, pair)
                    add_expert(q, pair)

            dve.sem_inc(y_free, 2)
            split_lo(0, 0)
            with dve.Fori(0, EXPERTS // 2 - 1) as pair:
                expert_pair(pair, False)
            expert_pair(EXPERTS // 2 - 1, True)
            for b in range(BATCHES):
                dve.wait_ge(final_ready, b + 1)
                flat = xs[:, b].rearrange("p t d -> p (t d)")
                nc.vector.tensor_tensor(flat, ps_final[:, b % 2], flat, ALU.add).then_inc(out_ready, 1)

        @block.gpsimd
        def _(pool):
            chain = [0]

            def link(ins):
                chain[0] += 1
                ins.then_inc(pool_chain, 1)
                pool.wait_ge(pool_chain, chain[0])

            link(nc.gpsimd.memset(minus_half[:, :], -0.5))
            link(nc.gpsimd.memset(ident[:, :], 0.0))
            nc.gpsimd.affine_select(out=ident[:, :], in_=ident[:, :], compare_op=ALU.not_equal, fill=1.0, base=0,
                                    pattern=[[-1, P]], channel_multiplier=1).then_inc(ident_ready, 1)
            link(nc.gpsimd.memset(causal[:, :], 0.0))
            tail = causal[:, SEQ - P:SEQ]
            nc.gpsimd.affine_select(out=tail, in_=tail, compare_op=ALU.is_ge, fill=MASKED, base=0,
                                    pattern=[[-1, P]], channel_multiplier=1).then_inc(causal_ready, 1)
            for g in range(GROUPS):
                nc.gpsimd.memset(q_stack[:, g].bitcast(F32), 0.0).then_inc(stacks_cleared, 1)
            nc.gpsimd.memset(v_ones[:, :, :, :], 0.0).then_inc(v_cleared, 1)
            pool.wait_ge(v_cleared, 1)
            nc.gpsimd.memset(v_ones[:, :, :, HD:HD + 1], 1.0).then_inc(v_cleared, 1)
            nc.gpsimd.iota(rank[:, :], [[-1, EXPERTS]], base=EXPERTS, channel_multiplier=0,
                           allow_small_or_imprecise_dtypes=True)
            nc.gpsimd.memset(acc[:, :, :], 0.0).then_inc(acc_done, 1)

            def split(src, hi, lo, signal):
                link(nc.gpsimd.tensor_scalar(hi, src, 1.0, 1.0, ALU.mult, ALU.mult))
                ins = nc.gpsimd.tensor_tensor(lo, src, hi.bitcast(F32), ALU.subtract)
                if signal is not None:
                    ins.then_inc(signal, 1)

            def split_expert(k):
                slot = k % 2
                pool.wait_ge(w12_loaded[slot], 16 * 2 * (k // 2 + 1))
                split(w1_in[:, slot], w1_hi[:, slot], w1_lo[:, slot], None)
                flat = lambda w: w[:, slot].rearrange("p f d -> p (f d)")
                split(flat(w2_in), flat(w2_hi), flat(w2_lo), w12_split)

            ln = 0
            for stage, n, i in PLAN:
                if stage in ("ln1_stats", "project"):
                    ln += 1
                    pool.wait_ge(var_ready, ln)
                    nc.gpsimd.tensor_tensor(rstd[:, :], var_eps[:, :], minus_half[:, :], ALU.pow)\
                        .then_inc(rstd_ready, 1)
                elif stage == "shifted":
                    j, heads = SHIFTED[i]
                    if LAST_UNIT[j] == i:
                        pool.wait_ge(exp_done, NSH * n + i + 1)
                        diag = p_t[:, n % 2, PT_AT[j]:PT_AT[j] + R * PT_WIDTH[j]].rearrange(
                            "p (h q) -> p h q", h=R)[:, :, 0:P]
                        nc.gpsimd.affine_select(out=diag, in_=diag, compare_op=ALU.is_ge, fill=0.0, base=0,
                                                pattern=[[0, R], [1, P]], channel_multiplier=-1)\
                            .then_inc(causal_done, 1)
                elif stage == "x2_transpose":
                    pool.wait_ge(shared_drained, drained(stage, n))
                    split(x2n_t[:, :], x_hi[:, n], x_lo[:, n], x2_split)
                    if n < 2:
                        split_expert(n)
            for k in range(2, EXPERTS):
                split_expert(k)


def kernel(L0_attn_x, L0_attn_qw, L0_attn_kw, L0_attn_vw, L0_attn_ow,
           L0_ffn_W1, L0_ffn_b1, L0_ffn_W2, L0_ffn_b2, L0_ffn_Wg, L0_ffn_bg):
    import numpy as np
    import concourse.bacc as bacc
    from concourse.bass_utils import run_bass_kernel_spmd

    by_head = lambda w: np.asarray(w).reshape(P, HD, HEADS).transpose(0, 2, 1).reshape(P, P)
    arrays = {
        "x": L0_attn_x, "qw": by_head(L0_attn_qw), "kw": by_head(L0_attn_kw), "vw": L0_attn_vw, "ow": L0_attn_ow,
        "W1": L0_ffn_W1,
        "b1": np.asarray(L0_ffn_b1).reshape(EXPERTS, FT, P).transpose(0, 2, 1),
        "W2": L0_ffn_W2,
        "b2": np.asarray(L0_ffn_b2).reshape(EXPERTS, P, 1),
        "Wg": L0_ffn_Wg, "bg": L0_ffn_bg,
    }
    arrays = {name: np.ascontiguousarray(a) for name, a in arrays.items()}
    nc = bacc.Bacc("TRN2", target_bir_lowering=False, num_devices=1)
    args = [nc.dram_tensor(name, a.shape, F32, kind="ExternalInput").ap() for name, a in arrays.items()]
    out = nc.dram_tensor("out", (BATCHES, SEQ, P), F32, kind="ExternalOutput").ap()
    build(nc, *args, out)
    result = run_bass_kernel_spmd(nc, [arrays], core_ids=[0])
    return result.results[0]["out"]
```

```python
import math
from contextlib import ExitStack

import concourse.bass as bass
from concourse import mybir

F32 = mybir.dt.float32
F32R = mybir.dt.float32r
BF16 = mybir.dt.bfloat16
ALU = mybir.AluOpType
ACT = mybir.ActivationFunctionType
AX_X = mybir.AxisListType.X

P = 128
BATCHES, SEQ = 4, 512
TILES = SEQ // P
HEADS, HD = 16, 8
R = 4
GROUPS = HEADS // R
STEPS = BATCHES * GROUPS
EXPERTS, FF = 8, 512
FT = FF // P
SCALE = float(P) ** -0.5
EPS = 1e-5
MASKED = -1e30
LAG = 3
UNITS = BATCHES * FT
LAST_PAIR = EXPERTS // 2 - 1

PT_WIDTH = [SEQ - P * j for j in range(TILES)]
PT_AT = [R * sum(PT_WIDTH[:j]) for j in range(TILES)]
PT_SIZE = R * sum(PT_WIDTH)
SHIFTED = [(j, (r,)) for j in (0, 1) for r in range(R)] + [(j, pair) for j in (2, 3) for pair in ((0, 1), (2, 3))]
NSH = len(SHIFTED)
LAST_UNIT = {3: 0, 7: 1, 9: 2, 11: 3}
RING = 3
SCORES = [(r, t) for r in range(R) for t in range(TILES)]
NSC = len(SCORES)
SHIFTED_SLOT = {0: 0, 1: 1, 2: 2, 4: 3, 5: 4, 6: 5, 8: 6, 9: 7, 10: 8, 12: 9, 13: 10, 14: 11}
PV_SLOT = {1: 0, 3: 1, 5: 2, 7: 3}

FIRST_STEP = -4


def batch_at(n, offset):
    b, rest = divmod(n - offset, GROUPS)
    return b if rest == 0 and 0 <= b < BATCHES else None


def plan(n):
    valid = lambda k: 0 <= k < STEPS
    events = []

    def per_batch(name, offset):
        b = batch_at(n, offset)
        if b is not None:
            events.append((name, b, None))

    per_batch("ln2_normalise", 6)
    per_batch("ln1_stats", -4)
    if valid(n + 1):
        events.append(("max_transpose", n + 1, None))
    for slot in range(NSC):
        if valid(n + 2):
            events.append(("scores", n + 2, slot))
        if valid(n) and slot in SHIFTED_SLOT:
            events.append(("shifted", n, SHIFTED_SLOT[slot]))
        if valid(n - 1) and slot in PV_SLOT:
            events.append(("pv", n - 1, PV_SLOT[slot]))
        if slot == 1:
            per_batch("q_project", -3)
            per_batch("x2_transpose", 6)
        if slot == 3:
            per_batch("k_project", -3)
        if slot == 4 and valid(n - 2):
            events.append(("out_transpose", n - 2, None))
        if slot == 6:
            per_batch("ln1_normalise", -4)
        if slot == 8:
            per_batch("attn_transpose", 5)
        if slot == 9:
            per_batch("gate", 6)
        if slot == 13:
            per_batch("gate_finish", 6)
        if slot == 11:
            per_batch("weight_transpose", 7)
        if slot == 14:
            per_batch("v_project", 0)
            per_batch("project", 5)
        if slot == 15:
            per_batch("x_transpose", -4)
    return events


B3, S15 = BATCHES - 1, STEPS - 1
TAIL = {
    -3: [("pv", S15, 0)], -2: [("pv", S15, 1)], -1: [("out_transpose", S15 - 1, None), ("pv", S15, 2)],
    0: [("pv", S15, 3)], 1: [("out_transpose", S15, None)], 2: [("attn_transpose", B3, None)],
    3: [("project", B3, None)], 5: [("ln2_normalise", B3, None), ("x2_transpose", B3, None)],
    7: [("gate", B3, None)], 9: [("gate_finish", B3, None)], 11: [("weight_transpose", B3, None)],
}
MAIN = [e for n in range(FIRST_STEP, STEPS) for e in plan(n)]
PLAN = MAIN + [e for l in sorted(TAIL) for e in TAIL[l]]
SHARED = ("max_transpose", "q_project", "k_project", "x2_transpose", "out_transpose", "attn_transpose",
          "gate", "weight_transpose", "v_project", "project", "x_transpose")
LN_USE = {(e[0], e[1]): i + 1 for i, e in enumerate([e for e in PLAN if e[0] in ("ln1_normalise", "ln2_normalise")])}
SHARED_USE = {(e[0], e[1]): i for i, e in enumerate([e for e in PLAN if e[0] in SHARED])}


def peeled(pair, which):
    return isinstance(pair, int) and pair == which


def build(nc, x, qw, kw, vw, ow, W1, b1, W2, b2, Wg, bg, out):
    with ExitStack() as ctx:
        def sb(name, shape, dt=F32):
            return ctx.enter_context(nc.sbuf_tensor(name, shape, dt))

        def sem(name):
            return ctx.enter_context(nc.semaphore(name))

        q_planes = nc.dram_tensor("q_planes", (2, HEADS, 4, HD, SEQ), F32, kind="Internal").ap()
        k_planes = nc.dram_tensor("k_planes", (2, HEADS, 4, HD, SEQ), F32, kind="Internal").ap()
        weight_rows = nc.dram_tensor("weight_rows", (BATCHES, EXPERTS, SEQ), F32, kind="Internal").ap()

        ident = sb("ident", [P, P])
        causal = sb("causal", [P, SEQ])
        minus_half = sb("minus_half", [P, TILES])
        euler = sb("euler", [P, TILES])
        rank = sb("rank", [P, EXPERTS])
        plane_const = sb("plane_const", [P, 2, SEQ])
        qw_s, kw_s, vw_s, ow_s = (sb(n, [P, P]) for n in ("qw_s", "kw_s", "vw_s", "ow_s"))
        wg_s = sb("wg_s", [P, EXPERTS])
        bg_s = sb("bg_s", [P, EXPERTS])
        xs = sb("xs", [P, BATCHES, TILES, P])
        stats = sb("stats", [P, TILES, 6])
        moments = sb("moments", [P, TILES, 2])
        var_eps = sb("var_eps", [P, TILES])
        rstd = sb("rstd", [P, TILES])
        xn = sb("xn", [P, TILES, P])
        xn_t = sb("xn_t", [P, SEQ])
        qk_f = sb("qk_f", [P, 2, SEQ])
        q_hi, q_lo, k_hi, k_lo = (sb(n, [P, SEQ], F32R) for n in ("q_hi", "q_lo", "k_hi", "k_lo"))
        q_stack = sb("q_stack", [P, GROUPS, R, SEQ], F32R)
        k_stack = sb("k_stack", [P, GROUPS, SEQ], F32R)
        v_ones = sb("v_ones", [P, TILES, HEADS, 32])
        row_max = sb("row_max", [P, 2, R * TILES])
        neg_max = sb("neg_max", [R * TILES, 2, P], F32R)
        scratch = sb("scratch", [P, 4, SEQ], BF16)
        p_t = sb("p_t", [P, 2, PT_SIZE])
        pv_s = sb("pv_s", [P, 2, SEQ])
        rsum = sb("rsum", [P, TILES, R])
        attn = sb("attn", [P, TILES, P])
        attn_t = sb("attn_t", [P, SEQ])
        x2n = sb("x2n", [P, TILES, P])
        x2n_t = sb("x2n_t", [P, SEQ])
        x_hi = sb("x_hi", [P, BATCHES, SEQ], F32R)
        x_lo = sb("x_lo", [P, BATCHES, SEQ], F32R)
        gate_f = sb("gate_f", [P, 8, TILES, EXPERTS])
        gate_s = sb("gate_s", [P, 9, TILES])
        weights = sb("weights", [P, EXPERTS, TILES])
        weights_t = sb("weights_t", [EXPERTS * TILES, P])
        w1_in = sb("w1_in", [P, 2, FF])
        w2_in = sb("w2_in", [P, 2, FT, P])
        w1_hi, w1_lo = (sb(n, [P, 2, FF], F32R) for n in ("w1_hi", "w1_lo"))
        w2_hi, w2_lo = (sb(n, [P, 2, FT, P], F32R) for n in ("w2_hi", "w2_lo"))
        b1_s = sb("b1_s", [P, 2, FT])
        b2_s = sb("b2_s", [P, 2])
        y_w = sb("y_w", [P, SEQ])
        acc = sb("acc", [P, BATCHES, SEQ])
        act_f = p_t[:, 0, 0:FT * SEQ].rearrange("p (f t) -> p f t", f=FT)
        weight_bc = p_t[:, 1, 0:2 * BATCHES * SEQ].rearrange("p (e t) -> p e t", e=2)
        act_hi = k_stack
        act_lo = q_stack[:, 0]

        banks = ctx.enter_context(nc.psum_tensor("banks", [P, 8, SEQ], F32))
        ps_scores, ps_shifted = banks[:, 0:RING], banks[:, RING:2 * RING]
        ps_pv, ps_shared = banks[:, 6], banks[:, 7]
        ps_y, ps_h, ps_final = banks[:, 0:2], banks[:, 2:2 + FT], banks[:, 6:8]

        x0_loaded, x_loaded = sem("x0_loaded"), sem("x_loaded")
        w_loaded = sem("w_loaded")
        ident_ready, causal_ready, consts_ready = sem("ident_ready"), sem("causal_ready"), sem("consts_ready")
        stacks_cleared, v_cleared = sem("stacks_cleared"), sem("v_cleared")
        planes_cleared = sem("planes_cleared")
        dve_chain, pool_chain = sem("dve_chain"), sem("pool_chain")
        var_ready, rstd_ready = sem("var_ready"), sem("rstd_ready")
        xn_ready = sem("xn_ready")
        q_hi_ready, k_hi_ready = sem("q_hi_ready"), sem("k_hi_ready")
        planes_written = sem("planes_written")
        stack_loaded = [sem("stack_loaded_even"), sem("stack_loaded_odd")]
        max_loaded = [sem("max_loaded_even"), sem("max_loaded_odd")]
        scores_ready, max_done = sem("scores_ready"), sem("max_done")
        shared_filled, shared_drained = sem("shared_filled"), sem("shared_drained")
        shifted_ready, exp_done, causal_done = sem("shifted_ready"), sem("exp_done"), sem("causal_done")
        pv_done, pv_saved = sem("pv_done"), sem("pv_saved")
        x2n_ready, x2_split = sem("x2n_ready"), sem("x2_split")
        gap_ready, gap_exp = sem("gap_ready"), sem("gap_exp")
        weights_ready, weights_written = sem("weights_ready"), sem("weights_written")
        w12_loaded = [sem("w12_loaded_even"), sem("w12_loaded_odd")]
        bias_loaded = [sem("bias_loaded_even"), sem("bias_loaded_odd")]
        routing_loaded = [sem("routing_loaded_even"), sem("routing_loaded_odd")]
        w12_split = sem("w12_split")
        h_ready = sem("h_ready")
        act_done = sem("act_done")
        lo_done = sem("lo_done")
        unit_done = sem("unit_done")
        y_free = sem("y_free")
        acc_done = sem("acc_done")
        final_ready, out_ready, out_stored = sem("final_ready"), sem("out_ready"), sem("out_stored")

        filled = lambda stage, n: SHARED_USE[stage, n] + 1
        drained = filled

        x_tiles = x.rearrange("b (t p) d -> p b t d", p=P)
        out_tiles = out.rearrange("b (t p) d -> p b t d", p=P)
        expert_of = lambda k: 2 * k if k < EXPERTS // 2 else 2 * (k - EXPERTS // 2) + 1

        block = ctx.enter_context(nc.Block())

        @block.sync
        def _(sp):
            sp.dma_start(xs[:, 0], x_tiles[:, 0]).then_inc(x0_loaded, 16)
            for dst, src in ((qw_s, qw), (kw_s, kw), (vw_s, vw), (ow_s, ow), (wg_s, Wg)):
                sp.dma_start(dst[:, :], src).then_inc(w_loaded, 16)
            sp.dma_start(bg_s[:, :], bg.rearrange("(a e) -> a e", a=1).to_broadcast([P, EXPERTS])).then_inc(w_loaded, 16)
            sp.wait_ge(consts_ready, 1)
            for par in range(2):
                for planes, c in ((q_planes, 0), (k_planes, 1)):
                    sp.dma_start(planes[par].rearrange("h c i t -> c h (i t)")[3],
                                 plane_const[:, c]).then_inc(planes_cleared, 16)
            sp.dma_start(xs[:, 1:], x_tiles[:, 1:]).then_inc(x_loaded, 16)

            def load_expert(k):
                e, slot = expert_of(k), k % 2
                if k >= 2:
                    sp.wait_ge(acc_done, 1 + BATCHES * (k - 1))
                sp.dma_start(w1_in[:, slot], W1[e]).then_inc(w12_loaded[slot], 16)
                sp.dma_start(w2_in[:, slot], W2[e].rearrange("(f p) d -> p f d", p=P)).then_inc(w12_loaded[slot], 16)

            def load_bias(k):
                e, slot = expert_of(k), k % 2
                sp.dma_start(b1_s[:, slot], b1[e]).then_inc(bias_loaded[slot], 16)
                sp.dma_start(b2_s[:, slot:slot + 1], b2[e]).then_inc(bias_loaded[slot], 16)

            def load_routing(k, batches):
                e, slot = expert_of(k), k % 2
                src = weight_rows[:, e]
                dst = weight_bc[:, slot].rearrange("p (b t) -> p b t", b=BATCHES)
                for b in batches:
                    sp.dma_start(dst[:, b], src[b:b + 1].to_broadcast([P, SEQ])).then_inc(routing_loaded[slot], 16)

            def load_stacks(n):
                b, g = divmod(n, GROUPS)
                if n == 0:
                    sp.wait_ge(planes_cleared, 16 * 4)
                if n < GROUPS:
                    sp.wait_ge(stacks_cleared, n + 1)
                if g == 0:
                    sp.wait_ge(planes_written, 16 * 6 * (b + 1))
                if n >= GROUPS:
                    sp.wait_ge(shifted_ready, NSH * (n - GROUPS + 1))
                for r in range(R):
                    sp.dma_start(q_stack[32 * r:32 * r + 32, g, r].bitcast(F32),
                                 q_planes[b % 2][R * g + r].rearrange("c i t -> (c i) t"))\
                        .then_inc(stack_loaded[n % 2], 16)
                sp.dma_start(k_stack[:, g].bitcast(F32),
                             k_planes[b % 2][R * g:R * g + R].rearrange("r c i t -> (r c i) t"))\
                    .then_inc(stack_loaded[n % 2], 16)

            for k in range(2):
                load_expert(k)
                load_bias(k)
            for stage, n, i in PLAN:
                if stage == "max_transpose":
                    sp.wait_ge(shared_drained, drained(stage, n))
                    for r in range(R):
                        row = 32 * r + 3 * HD
                        sp.dma_start(q_stack[row:row + 1, n % GROUPS, r].bitcast(F32),
                                     neg_max[r * TILES:(r + 1) * TILES, n % 2].bitcast(F32))\
                            .then_inc(max_loaded[n % 2], 16)
                if stage == "k_project":
                    b, par = n, n % 2
                    if b >= 2:
                        sp.wait_ge(stack_loaded[0], 16 * (R + 1) * 2 * (b - 1))
                        sp.wait_ge(stack_loaded[1], 16 * (R + 1) * 2 * (b - 1))
                    sp.wait_ge(shared_drained, drained("q_project", b))
                    q_dst = q_planes[par].rearrange("h c i t -> c h (i t)")
                    k_dst = k_planes[par].rearrange("h c i t -> c h (i t)")
                    for dst, src in ((q_dst[0], q_hi), (q_dst[1], q_hi), (q_dst[2], q_lo)):
                        sp.dma_start(dst, src[:, :].bitcast(F32)).then_inc(planes_written, 16)
                    sp.wait_ge(shared_drained, drained("k_project", b))
                    for dst, src in ((k_dst[0], k_hi), (k_dst[1], k_lo), (k_dst[2], k_hi)):
                        sp.dma_start(dst, src[:, :].bitcast(F32)).then_inc(planes_written, 16)
                    if b == 0:
                        load_stacks(0)
                if (stage, i) == ("scores", 5) and n + 1 < STEPS:
                    load_stacks(n + 1)
                if stage == "weight_transpose":
                    if n == BATCHES - 1:
                        sp.wait_ge(weights_written, 16 * n)
                        sp.wait_ge(pv_done, STEPS)
                        load_routing(0, range(n))
                    sp.wait_ge(shared_drained, drained(stage, n))
                    sp.dma_start(weight_rows[n].rearrange("e (q t) -> (e q) t", q=TILES), weights_t[:, :])\
                        .then_inc(weights_written, 16)
            sp.wait_ge(weights_written, 16 * BATCHES)
            sp.wait_ge(routing_loaded[0], 16 * (BATCHES - 1))
            load_routing(0, [BATCHES - 1])
            load_routing(1, range(BATCHES))
            for k in range(2, EXPERTS):
                load_expert(k)
                load_bias(k)
                load_routing(k, range(BATCHES))
            for b in range(BATCHES):
                sp.wait_ge(out_ready, b + 1)
                sp.dma_start(out_tiles[:, b], xs[:, b]).then_inc(out_stored, 16)
            sp.wait_ge(out_stored, 16 * BATCHES)

        @block.tensor
        def _(pe):
            def shared(stage, n):
                if SHARED_USE[stage, n]:
                    pe.wait_ge(shared_drained, SHARED_USE[stage, n])

            def attention(stage, n, i):
                if stage == "scores":
                    r, t = SCORES[i]
                    unit = NSC * n + i
                    if i == 0:
                        pe.wait_ge(stack_loaded[n % 2], 16 * (R + 1) * (n // 2 + 1))
                    if unit >= RING:
                        pe.wait_ge(max_done, unit + 1 - RING)
                    width = max(P * (t + 1), 2 * P)
                    nc.tensor.matmul(ps_scores[:, unit % RING, 0:width],
                                     q_stack[:, n % GROUPS, r, t * P:(t + 1) * P],
                                     k_stack[:, n % GROUPS, 0:width], start=True, stop=True)\
                        .then_inc(scores_ready, 1)
                elif stage == "max_transpose":
                    shared(stage, n)
                    pe.wait_ge(max_done, NSC * (n + 1))
                    nc.tensor.transpose(ps_shared[0:R * TILES, 0:P], row_max[:, n % 2], ident[:, :])\
                        .then_inc(shared_filled, 1)
                elif stage == "shifted":
                    j, heads = SHIFTED[i]
                    unit = NSH * n + i
                    if i == 0:
                        pe.wait_ge(max_loaded[n % 2], 16 * R * (n // 2 + 1))
                    if unit >= RING:
                        pe.wait_ge(exp_done, unit + 1 - RING)
                    q0 = min(P * j, SEQ - 2 * P)
                    for at, r in enumerate(heads):
                        col = at * (SEQ - q0)
                        last = nc.tensor.matmul(ps_shifted[:, unit % RING, col:col + SEQ - q0],
                                                k_stack[:, n % GROUPS, j * P:(j + 1) * P],
                                                q_stack[:, n % GROUPS, r, q0:SEQ], start=True, stop=True,
                                                skip_group_check=True)
                    last.then_inc(shifted_ready, 1)
                elif stage == "pv":
                    j = i
                    pe.wait_ge(causal_done, TILES * n + j + 1)
                    if j == 0:
                        pe.wait_ge(shared_drained, drained("v_project", n // GROUPS))
                        if n:
                            pe.wait_ge(pv_saved, n)
                    for r in range(R):
                        at = PT_AT[j] + r * PT_WIDTH[j]
                        last = nc.tensor.matmul(ps_pv[32 * r:32 * r + 32, j * P:SEQ],
                                                v_ones[:, j, R * (n % GROUPS) + r],
                                                p_t[:, n % 2, at:at + PT_WIDTH[j]],
                                                start=(j == 0), stop=(j == TILES - 1), skip_group_check=True)
                    if j == TILES - 1:
                        last.then_inc(pv_done, 1)
                elif stage == "out_transpose":
                    shared(stage, n)
                    pe.wait_ge(pv_saved, n + 1)
                    for t in range(TILES):
                        last = nc.tensor.transpose(ps_shared[:, t * P:(t + 1) * P],
                                                   pv_s[:, n % 2, t * P:(t + 1) * P], ident[:, :])
                    last.then_inc(shared_filled, 1)
                elif stage in ("x_transpose", "attn_transpose", "x2_transpose"):
                    shared(stage, n)
                    ready, count, src = {"x_transpose": (xn_ready, n + 1, xn),
                                         "attn_transpose": (shared_drained, SHARED_USE[stage, n], attn),
                                         "x2_transpose": (x2n_ready, n + 1, x2n)}[stage]
                    pe.wait_ge(ready, count)
                    for t in range(TILES):
                        last = nc.tensor.transpose(ps_shared[:, t * P:(t + 1) * P], src[:, t], ident[:, :])
                    last.then_inc(shared_filled, 1)
                elif stage in ("q_project", "k_project"):
                    shared(stage, n)
                    if n == 0:
                        pe.wait_ge(w_loaded, 16 * 6)
                    w = qw_s if stage == "q_project" else kw_s
                    nc.tensor.matmul(ps_shared, w[:, :], xn_t[:, :], start=True, stop=True)\
                        .then_inc(shared_filled, 1)
                elif stage == "v_project":
                    shared(stage, n)
                    for t in range(TILES):
                        last = nc.tensor.matmul(ps_shared[:, t * P:(t + 1) * P], xn_t[:, t * P:(t + 1) * P],
                                                vw_s[:, :], start=True, stop=True, skip_group_check=True)
                    last.then_inc(shared_filled, 1)
                elif stage == "project":
                    shared(stage, n)
                    for t in range(TILES):
                        last = nc.tensor.matmul(ps_shared[:, t * P:(t + 1) * P], attn_t[:, t * P:(t + 1) * P],
                                                ow_s[:, :], start=True, stop=True, skip_group_check=True)
                    last.then_inc(shared_filled, 1)
                elif stage == "gate":
                    shared(stage, n)
                    for t in range(TILES):
                        last = nc.tensor.matmul(ps_shared[:, t * EXPERTS:(t + 1) * EXPERTS],
                                                x2n_t[:, t * P:(t + 1) * P], wg_s[:, :],
                                                start=True, stop=True, skip_group_check=True)
                    last.then_inc(shared_filled, 1)
                elif stage == "weight_transpose":
                    shared(stage, n)
                    pe.wait_ge(weights_ready, n + 1)
                    nc.tensor.transpose(ps_shared[0:EXPERTS * TILES, 0:P],
                                        weights[:, :, :].rearrange("p e t -> p (e t)"), ident[:, :])\
                        .then_inc(shared_filled, 1)

            def up(local, pair):
                unit = UNITS * 2 * pair + local
                k2, b, f = (local // UNITS) % 2, (local // FT) % BATCHES, local % FT
                if local % UNITS == 0:
                    pe.wait_ge(w12_split, 2 * pair + local // UNITS + 1)
                if peeled(pair, 0) and local < UNITS and f == 0:
                    pe.wait_ge(x2_split, b + 1)
                pe.wait_ge(act_done, 2 * unit + 2)
                cols = slice(f * P, (f + 1) * P)
                for i, (w, xx) in enumerate(((w1_hi, x_hi), (w1_hi, x_lo), (w1_lo, x_hi))):
                    last = nc.tensor.matmul(ps_h[:, f], w[:, k2, cols], xx[:, b], start=(i == 0), stop=(i == 2))
                last.then_inc(h_ready, 1)

            def down(local, pair):
                unit = UNITS * 2 * pair + local
                k2, b, f = local // UNITS, (local // FT) % BATCHES, local % FT
                pe.wait_ge(lo_done, unit + 1)
                if f == 0:
                    pe.wait_ge(y_free, 2 * BATCHES * pair + local // FT + 1)
                for i, (w, aa) in enumerate(((w2_hi, act_hi), (w2_hi, act_lo), (w2_lo, act_hi))):
                    last = nc.tensor.matmul(ps_y[:, (local // FT) % 2], w[:, k2, f], aa[:, f],
                                            start=(f == 0 and i == 0), stop=(f == FT - 1 and i == 2))
                last.then_inc(unit_done, 1)

            pe.wait_ge(ident_ready, 1)
            for event in MAIN:
                attention(*event)
            pe.sem_inc(unit_done, FT)
            for local in range(-LAG, 2 * UNITS):
                for event in TAIL.get(local, ()):
                    attention(*event)
                if local == -LAG:
                    pe.wait_ge(exp_done, NSH * STEPS)
                if local >= 0:
                    down(local, 0)
                up(local + LAG, 0)
            with pe.Fori(1, LAST_PAIR) as pair:
                for local in range(2 * UNITS):
                    down(local, pair)
                    up(local + LAG, pair)
            for local in range(2 * UNITS):
                down(local, LAST_PAIR)
                if local + LAG < 2 * UNITS:
                    up(local + LAG, LAST_PAIR)
            for b in range(BATCHES):
                pe.wait_ge(acc_done, 1 + (EXPERTS - 1) * BATCHES + b + 1)
                if b >= 2:
                    pe.wait_ge(out_ready, b - 1)
                for t in range(TILES):
                    last = nc.tensor.transpose(ps_final[:, b % 2, t * P:(t + 1) * P],
                                               acc[:, b, t * P:(t + 1) * P], ident[:, :])
                last.then_inc(final_ready, 1)

        @block.scalar
        def _(act):
            def from_shared(stage, n, dst, src, signal=shared_drained, scale=1.0):
                act.wait_ge(shared_filled, filled(stage, n))
                nc.scalar.activation(dst, src, ACT.Copy, scale=scale).then_inc(signal, 1)

            def attention(stage, n, i):
                if stage == "max_transpose":
                    if n >= 2:
                        act.wait_ge(max_loaded[n % 2], 16 * R * (n // 2))
                    from_shared(stage, n, neg_max[:, n % 2], ps_shared[0:R * TILES, 0:P], scale=-1.0)
                elif stage == "shifted":
                    j, heads = SHIFTED[i]
                    unit = NSH * n + i
                    act.wait_ge(shifted_ready, unit + 1)
                    if i == 0 and n >= 2:
                        act.wait_ge(pv_done, n - 1)
                    width = PT_WIDTH[j]
                    at = PT_AT[j] + heads[0] * width
                    made = max(width, 2 * P)
                    src = ps_shifted[:, unit % RING, 0:len(heads) * made].rearrange(
                        "p (h q) -> p h q", q=made)[:, :, made - width:made]
                    nc.scalar.activation(
                        p_t[:, n % 2, at:at + len(heads) * width].rearrange("p (h q) -> p h q", q=width),
                        src, ACT.Exp, scale=SCALE).then_inc(exp_done, 1)
                elif stage == "pv" and i == TILES - 1:
                    act.wait_ge(pv_done, n + 1)
                    if n >= 2:
                        act.wait_ge(shared_filled, filled("out_transpose", n - 2))
                    nc.scalar.activation(pv_s[:, n % 2], ps_pv, ACT.Copy).then_inc(pv_saved, 1)
                elif stage == "x_transpose":
                    from_shared(stage, n, xn_t[:, :], ps_shared)
                elif stage == "q_project":
                    if n:
                        act.wait_ge(planes_written, 16 * 6 * n)
                    from_shared(stage, n, q_hi[:, :], ps_shared, q_hi_ready)
                elif stage == "k_project":
                    from_shared(stage, n, k_hi[:, :], ps_shared, k_hi_ready)
                elif stage == "v_project":
                    act.wait_ge(v_cleared, 2)
                    from_shared(stage, n, v_ones[:, :, :, 0:HD].rearrange("p t h i -> p t i h"),
                                ps_shared.rearrange("p (t i h) -> p t i h", t=TILES, i=HD))
                elif stage == "attn_transpose":
                    from_shared(stage, n, attn_t[:, :], ps_shared)
                elif stage == "x2_transpose":
                    if n:
                        act.wait_ge(x2_split, n)
                    from_shared(stage, n, x2n_t[:, :], ps_shared)
                elif stage == "weight_transpose":
                    if n:
                        act.wait_ge(weights_written, 16 * n)
                    from_shared(stage, n, weights_t[:, :], ps_shared[0:EXPERTS * TILES, 0:P])

            def activate(local, pair, func):
                unit = UNITS * 2 * pair + local
                slot, f = local // UNITS, local % FT
                if local % UNITS == 0:
                    act.wait_ge(bias_loaded[slot], 16 * 2 * (pair + 1))
                act.wait_ge(h_ready, unit + 1)
                act.wait_ge(unit_done, unit + 1)
                for dst in (act_f, act_hi):
                    nc.scalar.activation(dst[:, f], ps_h[:, f], func, bias=b1_s[:, slot, f:f + 1])\
                        .then_inc(act_done, 1)

            for event in MAIN:
                attention(*event)
            act.sem_inc(act_done, 2 * FT)
            for local in range(2 * UNITS):
                for event in TAIL.get(local - LAG, ()):
                    attention(*event)
                activate(local, 0, ACT.Gelu)
            for func, first, end in ((ACT.Gelu, 1, EXPERTS // 4), (ACT.Silu, EXPERTS // 4, EXPERTS // 2)):
                with act.Fori(first, end) as pair:
                    for local in range(2 * UNITS):
                        activate(local, pair, func)

        @block.vector
        def _(dve):
            chain = [0]

            def link(ins):
                chain[0] += 1
                ins.then_inc(dve_chain, 1)
                dve.wait_ge(dve_chain, chain[0])

            nc.vector.memset(plane_const[:, 0], 0.0)
            nc.vector.memset(plane_const[:, 1], 1.0).then_inc(consts_ready, 1)

            def ln_stats(src):
                for t in range(TILES):
                    last = nc.vector.bn_stats(stats[:, t], src[:, t])
                link(last)
                for t in range(TILES):
                    last = nc.vector.bn_aggr(moments[:, t], stats[:, t])
                link(last)
                nc.vector.tensor_scalar(var_eps[:, :], moments[:, :, 1], EPS, None, ALU.add).then_inc(var_ready, 1)

            def ln_normalise(dst, src, ready, count):
                dve.wait_ge(rstd_ready, count)
                for t in range(TILES):
                    last = nc.vector.tensor_scalar(dst[:, t], src[:, t], moments[:, t, 0:1], rstd[:, t:t + 1],
                                                   ALU.subtract, ALU.mult)
                last.then_inc(ready, 1)

            per_expert = lambda s: s.unsqueeze(2).to_broadcast([P, TILES, EXPERTS])
            per_tile = lambda s: s[:, :].unsqueeze(1).to_broadcast([P, TILES, EXPERTS])

            def first_largest(values, top, chosen, equal, ranked, best):
                link(nc.vector.tensor_reduce(top, values, AX_X, ALU.max))
                link(nc.vector.tensor_tensor(equal, values, per_expert(top), ALU.is_equal))
                link(nc.vector.tensor_tensor(ranked, equal, per_tile(rank), ALU.mult))
                link(nc.vector.tensor_reduce(best, ranked, AX_X, ALU.max))
                link(nc.vector.tensor_tensor(chosen, ranked, per_expert(best), ALU.is_equal))

            logits, equal, ranked, first, others, second, part_1, part_2 = (gate_f[:, i] for i in range(8))
            top_1, best, top_2, _, gap, gap_e, total, share_1, share_2 = (gate_s[:, i] for i in range(9))

            def attention(stage, n, i):
                if stage == "ln1_stats":
                    dve.wait_ge(x_loaded, 16) if n else dve.wait_ge(x0_loaded, 16)
                    ln_stats(xs[:, n])
                elif stage == "ln1_normalise":
                    if n:
                        dve.wait_ge(shared_filled, filled("x_transpose", n - 1))
                    ln_normalise(xn, xs[:, n], xn_ready, LN_USE[stage, n])
                elif stage == "ln2_normalise":
                    if n:
                        dve.wait_ge(shared_filled, filled("x2_transpose", n - 1))
                    ln_normalise(x2n, xs[:, n], x2n_ready, LN_USE[stage, n])
                elif stage == "scores":
                    r, t = SCORES[i]
                    unit = NSC * n + i
                    if i == 0:
                        dve.wait_ge(causal_ready, 1)
                        if n >= 2:
                            dve.wait_ge(shared_filled, filled("max_transpose", n - 2))
                    dve.wait_ge(scores_ready, unit + 1)
                    if unit >= 4:
                        dve.wait_ge(max_done, unit - 3)
                    width = P * (t + 1)
                    col = r * TILES + t
                    nc.vector.tensor_tensor_reduce(
                        out=scratch[:, unit % 4, 0:width], in0=ps_scores[:, unit % RING, 0:width],
                        in1=causal[:, SEQ - width:SEQ], scale=1.0, scalar=MASKED, op0=ALU.add, op1=ALU.max,
                        accum_out=row_max[:, n % 2, col:col + 1]).then_inc(max_done, 1)
                elif stage in ("q_project", "k_project"):
                    hi, lo, ready = (q_hi, q_lo, q_hi_ready) if stage == "q_project" else (k_hi, k_lo, k_hi_ready)
                    dve.wait_ge(ready, n + 1)
                    nc.vector.tensor_tensor(lo[:, :], ps_shared, hi[:, :].bitcast(F32), ALU.subtract)\
                        .then_inc(shared_drained, 1)
                elif stage == "out_transpose":
                    dve.wait_ge(shared_filled, filled(stage, n))
                    b, g = divmod(n, GROUPS)
                    if g == 0 and b:
                        dve.wait_ge(shared_filled, filled("attn_transpose", b - 1))
                    heads = ps_shared.rearrange("p (t r c) -> p t r c", t=TILES, c=32)
                    link(nc.vector.reciprocal(rsum[:, :, :], heads[:, :, :, HD]))
                    nc.vector.tensor_tensor(
                        attn[:, :, :].rearrange("p t (i g r) -> p t g r i", i=HD, g=GROUPS)[:, :, g],
                        heads[:, :, :, 0:HD], rsum[:, :, :].unsqueeze(3).to_broadcast([P, TILES, R, HD]),
                        ALU.mult).then_inc(shared_drained, 1)
                elif stage == "project":
                    dve.wait_ge(shared_filled, filled(stage, n))
                    flat = xs[:, n].rearrange("p t d -> p (t d)")
                    nc.vector.tensor_tensor(flat, ps_shared, flat, ALU.add).then_inc(shared_drained, 1)
                    dve.wait_ge(shared_drained, drained(stage, n))
                    ln_stats(xs[:, n])
                elif stage == "gate":
                    dve.wait_ge(shared_filled, filled(stage, n))
                    if n:
                        dve.wait_ge(weights_ready, n)
                    else:
                        dve.wait_ge(w_loaded, 16 * 6)
                    nc.vector.tensor_tensor(
                        logits, ps_shared[:, 0:TILES * EXPERTS].rearrange("p (t e) -> p t e", t=TILES),
                        per_tile(bg_s), ALU.add).then_inc(shared_drained, 1)
                    dve.wait_ge(shared_drained, drained(stage, n))
                    first_largest(logits, top_1, first, equal, ranked, best)
                    link(nc.vector.scalar_tensor_tensor(out=others, in0=first, scalar=MASKED, in1=logits,
                                                        op0=ALU.mult, op1=ALU.add))
                    first_largest(others, top_2, second, equal, ranked, best)
                    nc.vector.tensor_tensor(gap, top_2, top_1, ALU.subtract).then_inc(gap_ready, 1)
                elif stage == "gate_finish":
                    dve.wait_ge(gap_exp, n + 1)
                    link(nc.vector.tensor_scalar(total, gap_e, 1.0, None, ALU.add))
                    link(nc.vector.reciprocal(share_1, total))
                    link(nc.vector.tensor_tensor(share_2, gap_e, share_1, ALU.mult))
                    link(nc.vector.tensor_tensor(part_1, first, per_expert(share_1), ALU.mult))
                    link(nc.vector.tensor_tensor(part_2, second, per_expert(share_2), ALU.mult))
                    if n:
                        dve.wait_ge(shared_filled, filled("weight_transpose", n - 1))
                    nc.vector.tensor_tensor(weights[:, :, :].rearrange("p e t -> p t e"), part_1, part_2, ALU.add)\
                        .then_inc(weights_ready, 1)

            def split_lo(local, pair):
                f = local % FT
                dve.wait_ge(act_done, 2 * (2 * UNITS * pair + local + 1) + 2 * FT)
                nc.vector.tensor_tensor(act_lo[:, f], act_f[:, f], act_hi[:, f].bitcast(F32), ALU.subtract)\
                    .then_inc(lo_done, 1)

            def add_expert(q, pair):
                slot, b = q // BATCHES, q % BATCHES
                done = 2 * BATCHES * pair + q
                if q % BATCHES == 0:
                    dve.wait_ge(bias_loaded[slot], 16 * 2 * (pair + 1))
                if peeled(pair, 0) and q in (0, BATCHES - 1):
                    dve.wait_ge(routing_loaded[0], 16 * (BATCHES - 1 if q == 0 else BATCHES))
                elif q % BATCHES == 0:
                    dve.wait_ge(routing_loaded[slot], 16 * BATCHES * (pair + 1))
                dve.wait_ge(unit_done, FT * (done + 1) + FT)
                dve.wait_ge(acc_done, done + 1)
                nc.vector.scalar_tensor_tensor(
                    out=y_w[:, :], in0=ps_y[:, q % 2], scalar=b2_s[:, slot:slot + 1],
                    in1=weight_bc[:, slot, b * SEQ:(b + 1) * SEQ], op0=ALU.add, op1=ALU.mult).then_inc(y_free, 1)
                dve.wait_ge(y_free, done + 1 + 2)
                nc.vector.tensor_tensor(acc[:, b], acc[:, b], y_w[:, :], ALU.add).then_inc(acc_done, 1)

            def expert_unit(local, pair):
                if local + 1 < 2 * UNITS or not peeled(pair, LAST_PAIR):
                    split_lo(local + 1, pair)
                if local >= 0 and local % FT == FT - 1:
                    add_expert(local // FT, pair)

            for event in MAIN:
                attention(*event)
            dve.sem_inc(y_free, 2)
            for local in range(-LAG, 2 * UNITS):
                for event in TAIL.get(local, ()):
                    attention(*event)
                if local >= -1:
                    expert_unit(local, 0)
            with dve.Fori(1, LAST_PAIR) as pair:
                for local in range(2 * UNITS):
                    expert_unit(local, pair)
            for local in range(2 * UNITS):
                expert_unit(local, LAST_PAIR)
            for b in range(BATCHES):
                dve.wait_ge(final_ready, b + 1)
                flat = xs[:, b].rearrange("p t d -> p (t d)")
                nc.vector.tensor_tensor(flat, ps_final[:, b % 2], flat, ALU.add).then_inc(out_ready, 1)

        @block.gpsimd
        def _(pool):
            chain = [0]

            def link(ins):
                chain[0] += 1
                ins.then_inc(pool_chain, 1)
                pool.wait_ge(pool_chain, chain[0])

            link(nc.gpsimd.memset(minus_half[:, :], -0.5))
            link(nc.gpsimd.memset(euler[:, :], math.e))
            link(nc.gpsimd.memset(ident[:, :], 0.0))
            nc.gpsimd.affine_select(out=ident[:, :], in_=ident[:, :], compare_op=ALU.not_equal, fill=1.0, base=0,
                                    pattern=[[-1, P]], channel_multiplier=1).then_inc(ident_ready, 1)
            link(nc.gpsimd.memset(causal[:, :], 0.0))
            tail = causal[:, SEQ - P:SEQ]
            nc.gpsimd.affine_select(out=tail, in_=tail, compare_op=ALU.is_ge, fill=MASKED, base=0,
                                    pattern=[[-1, P]], channel_multiplier=1).then_inc(causal_ready, 1)
            for g in range(GROUPS):
                nc.gpsimd.memset(q_stack[:, g].bitcast(F32), 0.0).then_inc(stacks_cleared, 1)
            nc.gpsimd.memset(v_ones[:, :, :, :], 0.0).then_inc(v_cleared, 1)
            pool.wait_ge(v_cleared, 1)
            nc.gpsimd.memset(v_ones[:, :, :, HD:HD + 1], 1.0).then_inc(v_cleared, 1)
            nc.gpsimd.iota(rank[:, :], [[-1, EXPERTS]], base=EXPERTS, channel_multiplier=0,
                           allow_small_or_imprecise_dtypes=True)
            nc.gpsimd.memset(acc[:, :, :], 0.0).then_inc(acc_done, 1)

            def split(src, hi, lo, signal):
                link(nc.gpsimd.tensor_scalar(hi, src, 1.0, 1.0, ALU.mult, ALU.mult))
                ins = nc.gpsimd.tensor_tensor(lo, src, hi.bitcast(F32), ALU.subtract)
                if signal is not None:
                    ins.then_inc(signal, 1)

            def split_expert(k):
                slot = k % 2
                pool.wait_ge(w12_loaded[slot], 16 * 2 * (k // 2 + 1))
                split(w1_in[:, slot], w1_hi[:, slot], w1_lo[:, slot], None)
                flat = lambda w: w[:, slot].rearrange("p f d -> p (f d)")
                split(flat(w2_in), flat(w2_hi), flat(w2_lo), w12_split)

            ln = 0
            for stage, n, i in PLAN:
                if stage in ("ln1_stats", "project"):
                    ln += 1
                    pool.wait_ge(var_ready, ln)
                    nc.gpsimd.tensor_tensor(rstd[:, :], var_eps[:, :], minus_half[:, :], ALU.pow)\
                        .then_inc(rstd_ready, 1)
                elif stage == "shifted":
                    j, heads = SHIFTED[i]
                    if i in LAST_UNIT:
                        pool.wait_ge(exp_done, NSH * n + i + 1)
                        diag = p_t[:, n % 2, PT_AT[j]:PT_AT[j] + R * PT_WIDTH[j]].rearrange(
                            "p (h q) -> p h q", h=R)[:, :, 0:P]
                        nc.gpsimd.affine_select(out=diag, in_=diag, compare_op=ALU.is_ge, fill=0.0, base=0,
                                                pattern=[[0, R], [1, P]], channel_multiplier=-1)\
                            .then_inc(causal_done, 1)
                elif stage == "gate":
                    pool.wait_ge(gap_ready, n + 1)
                    nc.gpsimd.tensor_tensor(gate_s[:, 5], euler[:, :], gate_s[:, 4], ALU.pow).then_inc(gap_exp, 1)
                elif stage == "x2_transpose":
                    pool.wait_ge(shared_drained, drained(stage, n))
                    split(x2n_t[:, :], x_hi[:, n], x_lo[:, n], x2_split)
                    if n < 2:
                        split_expert(n)
            for k in range(2, EXPERTS):
                split_expert(k)


def kernel(L0_attn_x, L0_attn_qw, L0_attn_kw, L0_attn_vw, L0_attn_ow,
           L0_ffn_W1, L0_ffn_b1, L0_ffn_W2, L0_ffn_b2, L0_ffn_Wg, L0_ffn_bg):
    import numpy as np
    import concourse.bacc as bacc
    from concourse.bass_utils import run_bass_kernel_spmd

    by_head = lambda w: np.asarray(w).reshape(P, HD, HEADS).transpose(0, 2, 1).reshape(P, P)
    arrays = {
        "x": L0_attn_x, "qw": by_head(L0_attn_qw), "kw": by_head(L0_attn_kw), "vw": L0_attn_vw, "ow": L0_attn_ow,
        "W1": L0_ffn_W1,
        "b1": np.asarray(L0_ffn_b1).reshape(EXPERTS, FT, P).transpose(0, 2, 1),
        "W2": L0_ffn_W2,
        "b2": np.asarray(L0_ffn_b2).reshape(EXPERTS, P, 1),
        "Wg": L0_ffn_Wg, "bg": L0_ffn_bg,
    }
    arrays = {name: np.ascontiguousarray(a) for name, a in arrays.items()}
    nc = bacc.Bacc("TRN2", target_bir_lowering=False, num_devices=1)
    args = [nc.dram_tensor(name, a.shape, F32, kind="ExternalInput").ap() for name, a in arrays.items()]
    out = nc.dram_tensor("out", (BATCHES, SEQ, P), F32, kind="ExternalOutput").ap()
    build(nc, *args, out)
    result = run_bass_kernel_spmd(nc, [arrays], core_ids=[0])
    return result.results[0]["out"]
```

```python
import math
from contextlib import ExitStack

import concourse.bass as bass
from concourse import mybir

F32 = mybir.dt.float32
F32R = mybir.dt.float32r
BF16 = mybir.dt.bfloat16
ALU = mybir.AluOpType
ACT = mybir.ActivationFunctionType
AX_X = mybir.AxisListType.X

P = 128
BATCHES, SEQ = 4, 512
TILES = SEQ // P
HEADS, HD = 16, 8
R = 4
GROUPS = HEADS // R
STEPS = BATCHES * GROUPS
EXPERTS, FF = 8, 512
FT = FF // P
SCALE = float(P) ** -0.5
EPS = 1e-5
MASKED = -1e30
LAG = 3
UNITS = BATCHES * FT
AHEAD_LO = 1
LAST_PAIR = EXPERTS // 2 - 1

PT_WIDTH = [SEQ - P * j for j in range(TILES)]
PT_AT = [R * sum(PT_WIDTH[:j]) for j in range(TILES)]
PT_SIZE = R * sum(PT_WIDTH)
SHIFTED = [(j, (r,)) for j in (0, 1) for r in range(R)] + [(2, (0, 1)), (2, (2, 3)), (3, (0, 1, 2, 3))]
NSH = len(SHIFTED)
LAST_UNIT = {3: 0, 7: 1, 9: 2, 10: 3}
RING = 3
SCORES = [(r, tiles) for r in range(R) for tiles in ((0, 1), (2,), (3,))]
NSC = len(SCORES)
SCORES_BEFORE = [sum(len(tiles) for _, tiles in SCORES[:i]) for i in range(NSC + 1)]
NMAX = SCORES_BEFORE[NSC]
AHEAD = 4
PV_SLOT = {0: 0, 2: 1, 5: 2, 8: 3}
CHOICES = 13

FIRST_STEP = -7


def batch_at(n, offset):
    b, rest = divmod(n - offset, GROUPS)
    return b if rest == 0 and 0 <= b < BATCHES else None


def plan(n):
    valid = lambda k: 0 <= k < STEPS
    events = []

    def per_batch(name, offset, *parts):
        b = batch_at(n, offset)
        if b is not None:
            events.extend((name, b, i) for i in parts or (None,))

    for slot in range(NSC):
        if slot == 3 and valid(n + 1):
            events.append(("max_transpose", n + 1, None))
        if valid(n + 2):
            events.append(("scores", n + 2, slot))
        ahead_n, unit = divmod(NSC * n + slot + AHEAD, NSC)
        if valid(ahead_n) and unit < NSH:
            events.append(("shifted", ahead_n, unit))
        if valid(n - 1) and slot in PV_SLOT:
            events.append(("pv", n - 1, PV_SLOT[slot]))
        if slot == 4 and valid(n - 2):
            events.append(("out_transpose", n - 2, None))
        for name, offset, at, *parts in PER_BATCH:
            if slot == at:
                per_batch(name, offset, *parts)
    return events


PER_BATCH = [
    ("ln1_stats", -7, 0, 0), ("ln1_stats", -7, 1, 1), ("ln1_stats", -7, 2, 2), ("ln1_stats", -7, 3, 3),
    ("ln1_stats", -7, 4, 4), ("ln1_power", -7, 4), ("ln1_normalise", -7, 6, 0), ("ln1_normalise", -7, 7, 1),
    ("ln1_normalise", -7, 8, 2), ("ln1_normalise", -7, 9, 3),
    ("x_transpose", -4, 0), ("q_project", -4, 6), ("k_project", -4, 8), ("v_project", 0, 10),
    ("attn_transpose", 5, 7), ("project", 5, 9),
    ("ln2_stats", 5, 11, 0), ("ln2_stats", 6, 0, 1), ("ln2_stats", 6, 1, 2), ("ln2_stats", 6, 2, 3),
    ("ln2_stats", 6, 3, 4), ("ln2_power", 6, 3), ("ln2_normalise", 6, 5, 0), ("ln2_normalise", 6, 6, 1),
    ("ln2_normalise", 6, 7, 2), ("ln2_normalise", 6, 8, 3), ("x2_transpose", 6, 10), ("gate", 7, 0),
    ("choose", 7, 1, 0), ("choose", 7, 2, 1, 2), ("choose", 7, 3, 3, 4), ("choose", 7, 4, 5, 6),
    ("choose", 7, 5, 7, 8), ("choose", 7, 6, 9, 10), ("choose", 7, 7, 11, 12),
    ("gap_power", 7, 7), ("share", 8, 0, 0, 1), ("share", 8, 1, 2), ("share", 8, 2, 3), ("share", 8, 3, 4),
    ("weight_transpose", 8, 5),
]
FINAL_AT = {UNITS + FT * (b + 1) + 1: b for b in range(BATCHES - 1)}
B3, S15 = BATCHES - 1, STEPS - 1
TAIL = {
    -3: [("pv", S15, j) for j in range(TILES)] + [("share", B3 - 1, i) for i in range(5)],
    -2: [("out_transpose", S15 - 1, None), ("weight_transpose", B3 - 1, None)],
    -1: [("out_transpose", S15, None)],
    0: [("attn_transpose", B3, None)],
    1: [("project", B3, None)] + [("ln2_stats", B3, i) for i in range(5)] + [("ln2_power", B3, None)],
    3: [("ln2_normalise", B3, i) for i in range(TILES)],
    5: [("x2_transpose", B3, None)],
    6: [("gate", B3, None)] + [("choose", B3, i) for i in range(3)],
    7: [("choose", B3, i) for i in (3, 4, 5)], 8: [("choose", B3, i) for i in (6, 7, 8)],
    9: [("choose", B3, i) for i in (9, 10, 11, 12)] + [("gap_power", B3, None)],
    11: [("share", B3, i) for i in range(5)],
    12: [("weight_transpose", B3, None)],
}
MAIN = [e for n in range(FIRST_STEP, STEPS) for e in plan(n)]
PLAN = MAIN + [e for l in sorted(TAIL) for e in TAIL[l]]
SHARED = ("max_transpose", "q_project", "k_project", "x2_transpose", "out_transpose", "attn_transpose",
          "gate", "weight_transpose", "v_project", "project", "x_transpose")
LN_USE = {(e[0][:3], e[1]): i + 1 for i, e in enumerate([e for e in PLAN if e[0].endswith("_power") and e[0] != "gap_power"])}
SHARED_USE = {(e[0], e[1]): i for i, e in enumerate([e for e in PLAN if e[0] in SHARED])}


def peeled(pair, which):
    return isinstance(pair, int) and pair == which


def build(nc, x, qw, kw, vw, ow, W1, b1, W2, b2, Wg, bg, out):
    with ExitStack() as ctx:
        def sb(name, shape, dt=F32):
            return ctx.enter_context(nc.sbuf_tensor(name, shape, dt))

        def sem(name):
            return ctx.enter_context(nc.semaphore(name))

        q_planes = nc.dram_tensor("q_planes", (2, HEADS, 3, HD, SEQ), F32, kind="Internal").ap()
        k_planes = nc.dram_tensor("k_planes", (2, HEADS, 4, HD, SEQ), F32, kind="Internal").ap()
        weight_rows = nc.dram_tensor("weight_rows", (BATCHES, EXPERTS, SEQ), F32, kind="Internal").ap()

        ident = sb("ident", [P, P])
        causal = sb("causal", [P, SEQ])
        minus_half = sb("minus_half", [P, TILES])
        euler = sb("euler", [P, TILES])
        rank = sb("rank", [P, EXPERTS])
        qw_s, kw_s, vw_s, ow_s = (sb(n, [P, P]) for n in ("qw_s", "kw_s", "vw_s", "ow_s"))
        wg_s = sb("wg_s", [P, EXPERTS])
        bg_s = sb("bg_s", [P, EXPERTS])
        xs = sb("xs", [P, BATCHES, TILES, P])
        stats = sb("stats", [P, TILES, 6])
        moments = sb("moments", [P, TILES, 2])
        var_eps = sb("var_eps", [P, TILES])
        rstd = sb("rstd", [P, TILES])
        xn = sb("xn", [P, TILES, P])
        xn_t = sb("xn_t", [P, 2, SEQ])
        qk_f = sb("qk_f", [P, 2, SEQ])
        q_hi, q_lo, k_hi, k_lo = (sb(n, [P, SEQ], F32R) for n in ("q_hi", "q_lo", "k_hi", "k_lo"))
        q_stack = sb("q_stack", [P, GROUPS, R, SEQ], F32R)
        k_stack = sb("k_stack", [P, GROUPS, SEQ], F32R)
        v_ones = sb("v_ones", [P, TILES, HEADS, 32])
        row_max = sb("row_max", [P, 2, R * TILES])
        neg_max = sb("neg_max", [R * TILES, 2, P], F32R)
        scratch = sb("scratch", [P, 4, SEQ], BF16)
        p_t = sb("p_t", [P, 2, PT_SIZE])
        pv_s = sb("pv_s", [P, 2, SEQ])
        rsum = sb("rsum", [P, TILES, R])
        attn = sb("attn", [P, TILES, P])
        attn_t = sb("attn_t", [P, SEQ])
        x2n = sb("x2n", [P, TILES, P])
        x2n_t = sb("x2n_t", [P, SEQ])
        x_hi = sb("x_hi", [P, BATCHES, SEQ], F32R)
        x_lo = sb("x_lo", [P, BATCHES, SEQ], F32R)
        gate_f = sb("gate_f", [P, 8, TILES, EXPERTS])
        gate_s = sb("gate_s", [P, 9, TILES])
        weights = sb("weights", [P, EXPERTS, TILES])
        weights_t = sb("weights_t", [EXPERTS * TILES, P])
        w1_in = sb("w1_in", [P, 2, FF])
        w2_in = sb("w2_in", [P, 2, FT, P])
        w1_hi, w1_lo = (sb(n, [P, 2, FF], F32R) for n in ("w1_hi", "w1_lo"))
        w2_hi, w2_lo = (sb(n, [P, 2, FT, P], F32R) for n in ("w2_hi", "w2_lo"))
        b1_s = sb("b1_s", [P, 2, FT])
        b2_s = sb("b2_s", [P, 2])
        y_w = sb("y_w", [P, SEQ])
        acc = sb("acc", [P, BATCHES, SEQ])
        act_f = p_t[:, 0, 0:FT * SEQ].rearrange("p (f t) -> p f t", f=FT)
        weight_bc = p_t[:, 1, 0:2 * BATCHES * SEQ].rearrange("p (e t) -> p e t", e=2)
        act_hi = k_stack
        act_lo = q_stack[:, 0]

        banks = ctx.enter_context(nc.psum_tensor("banks", [P, 8, SEQ], F32))
        ps_scores, ps_shifted = banks[:, 0:RING], banks[:, RING:2 * RING]
        ps_pv, ps_shared = banks[:, 6], banks[:, 7]
        ps_y, ps_h, ps_final = banks[:, 0:2], banks[:, 2:2 + FT], banks[:, 6:8]

        x0_loaded, x_loaded = sem("x0_loaded"), sem("x_loaded")
        w_loaded = sem("w_loaded")
        ident_ready, causal_ready, ones_ready = sem("ident_ready"), sem("causal_ready"), sem("ones_ready")
        stacks_cleared, v_cleared = sem("stacks_cleared"), sem("v_cleared")
        dve_chain, pool_chain = sem("dve_chain"), sem("pool_chain")
        var_ready, rstd_ready, normalised = sem("var_ready"), sem("rstd_ready"), sem("normalised")
        q_hi_ready, k_hi_ready = sem("q_hi_ready"), sem("k_hi_ready")
        qk_lo_ready = sem("qk_lo_ready")
        planes_set = sem("planes_set")
        q_written, k_written = sem("q_written"), sem("k_written")
        stack_loaded = [sem("stack_loaded_even"), sem("stack_loaded_odd")]
        max_loaded = [sem("max_loaded_even"), sem("max_loaded_odd")]
        scores_ready, max_done = sem("scores_ready"), sem("max_done")
        shared_filled, shared_drained = sem("shared_filled"), sem("shared_drained")
        shifted_ready, exp_done, causal_done = sem("shifted_ready"), sem("exp_done"), sem("causal_done")
        pv_done, pv_saved = sem("pv_done"), sem("pv_saved")
        x2_split = sem("x2_split")
        gap_ready, gap_exp = sem("gap_ready"), sem("gap_exp")
        weights_ready, weights_written = sem("weights_ready"), sem("weights_written")
        w12_loaded = [sem("w12_loaded_even"), sem("w12_loaded_odd")]
        bias_loaded = [sem("bias_loaded_even"), sem("bias_loaded_odd")]
        routing_loaded = [sem("routing_loaded_even"), sem("routing_loaded_odd")]
        w12_split = sem("w12_split")
        h_ready = sem("h_ready")
        act_done = sem("act_done")
        lo_done = sem("lo_done")
        unit_done = sem("unit_done")
        y_free = sem("y_free")
        acc_done = sem("acc_done")
        final_ready, out_ready, out_stored = sem("final_ready"), sem("out_ready"), sem("out_stored")

        filled = lambda stage, n: SHARED_USE[stage, n] + 1
        drained = filled
        maxima = lambda units: NMAX * (units // NSC) + SCORES_BEFORE[units % NSC]

        x_tiles = x.rearrange("b (t p) d -> p b t d", p=P)
        out_tiles = out.rearrange("b (t p) d -> p b t d", p=P)
        expert_of = lambda k: 2 * k if k < EXPERTS // 2 else 2 * (k - EXPERTS // 2) + 1

        block = ctx.enter_context(nc.Block())

        @block.sync
        def _(sp):
            sp.dma_start(xs[:, 0], x_tiles[:, 0]).then_inc(x0_loaded, 16)
            for dst, src in ((qw_s, qw), (kw_s, kw), (vw_s, vw), (ow_s, ow), (wg_s, Wg)):
                sp.dma_start(dst[:, :], src).then_inc(w_loaded, 16)
            sp.dma_start(xs[:, 1:], x_tiles[:, 1:]).then_inc(x_loaded, 16)
            sp.dma_start(bg_s[:, :], bg.rearrange("(a e) -> a e", a=1).to_broadcast([P, EXPERTS])).then_inc(w_loaded, 16)
            sp.wait_ge(ones_ready, 1)
            for par in range(2):
                sp.dma_start(k_planes[par].rearrange("h c i t -> c h (i t)")[3],
                             k_stack[:, GROUPS - 1].bitcast(F32)).then_inc(planes_set, 16)

            def load_expert(k):
                e, slot = expert_of(k), k % 2
                if k >= 2:
                    sp.wait_ge(acc_done, 1 + BATCHES * (k - 1))
                sp.dma_start(w1_in[:, slot], W1[e]).then_inc(w12_loaded[slot], 16)
                sp.dma_start(w2_in[:, slot], W2[e].rearrange("(f p) d -> p f d", p=P)).then_inc(w12_loaded[slot], 16)

            def load_bias(k):
                e, slot = expert_of(k), k % 2
                sp.dma_start(b1_s[:, slot], b1[e]).then_inc(bias_loaded[slot], 16)
                sp.dma_start(b2_s[:, slot:slot + 1], b2[e]).then_inc(bias_loaded[slot], 16)

            def load_routing(k, batches):
                e, slot = expert_of(k), k % 2
                src = weight_rows[:, e]
                dst = weight_bc[:, slot].rearrange("p (b t) -> p b t", b=BATCHES)
                for b in batches:
                    sp.dma_start(dst[:, b], src[b:b + 1].to_broadcast([P, SEQ])).then_inc(routing_loaded[slot], 16)

            def load_stacks(n):
                b, g = divmod(n, GROUPS)
                if n >= 2:
                    sp.wait_ge(scores_ready, NSC * (n - 2) + 1)
                if n < GROUPS:
                    sp.wait_ge(stacks_cleared, n + 1)
                    sp.wait_ge(planes_set, 16 * 2)
                if g == 0:
                    sp.wait_ge(q_written, 16 * 3 * (b + 1))
                if n >= GROUPS:
                    sp.wait_ge(shifted_ready, NSH * (n - GROUPS + 1))
                for r in range(R):
                    sp.dma_start(q_stack[32 * r:32 * r + 3 * HD, g, r].bitcast(F32),
                                 q_planes[b % 2][R * g + r].rearrange("c i t -> (c i) t"))\
                        .then_inc(stack_loaded[n % 2], 16)
                if g == 0:
                    sp.wait_ge(k_written, 16 * 3 * (b + 1))
                sp.dma_start(k_stack[:, g].bitcast(F32),
                             k_planes[b % 2][R * g:R * g + R].rearrange("r c i t -> (r c i) t"))\
                    .then_inc(stack_loaded[n % 2], 16)

            for stage, n, i in PLAN:
                if stage == "max_transpose":
                    sp.wait_ge(shared_drained, drained(stage, n))
                    sp.dma_start(q_stack[3 * HD:3 * HD + 1, n % GROUPS].bitcast(F32),
                                 neg_max[:, n % 2].bitcast(F32)).then_inc(max_loaded[n % 2], 16)
                if stage == "k_project":
                    b, par = n, n % 2
                    if b >= 2:
                        sp.wait_ge(stack_loaded[0], 16 * (R + 1) * 2 * (b - 1))
                        sp.wait_ge(stack_loaded[1], 16 * (R + 1) * 2 * (b - 1))
                    q_dst = q_planes[par].rearrange("h c i t -> c h (i t)")
                    k_dst = k_planes[par].rearrange("h c i t -> c h (i t)")
                    for ready, dst, hi, lo, hi_at, lo_at, lo_count, written in (
                            (q_hi_ready, q_dst, q_hi, q_lo, (0, 1), (2,), 2 * b + 1, q_written),
                            (k_hi_ready, k_dst, k_hi, k_lo, (0, 2), (1,), 2 * b + 2, k_written)):
                        sp.wait_ge(ready, b + 1)
                        for c in hi_at:
                            sp.dma_start(dst[c], hi[:, :].bitcast(F32)).then_inc(written, 16)
                        sp.wait_ge(qk_lo_ready, lo_count)
                        for c in lo_at:
                            sp.dma_start(dst[c], lo[:, :].bitcast(F32)).then_inc(written, 16)
                    if b == 0:
                        load_stacks(0)
                if (stage, i) == ("scores", 0) and n + 1 < STEPS:
                    load_stacks(n + 1)
                    if n < 2:
                        load_expert(n)
                        load_bias(n)
                if stage == "weight_transpose":
                    if n == BATCHES - 1:
                        sp.wait_ge(weights_written, 16 * n)
                        sp.wait_ge(pv_done, STEPS)
                        load_routing(0, range(n))
                    sp.wait_ge(shared_drained, drained(stage, n))
                    sp.dma_start(weight_rows[n].rearrange("e (q t) -> (e q) t", q=TILES), weights_t[:, :])\
                        .then_inc(weights_written, 16)
            sp.wait_ge(weights_written, 16 * BATCHES)
            sp.wait_ge(routing_loaded[0], 16 * (BATCHES - 1))
            load_routing(0, [BATCHES - 1])
            load_routing(1, range(BATCHES))
            for k in range(2, EXPERTS):
                load_expert(k)
                load_bias(k)
                load_routing(k, range(BATCHES))
            for b in range(BATCHES):
                sp.wait_ge(out_ready, b + 1)
                sp.dma_start(out_tiles[:, b], xs[:, b]).then_inc(out_stored, 16)
            sp.wait_ge(out_stored, 16 * BATCHES)

        @block.tensor
        def _(pe):
            def shared(stage, n):
                if SHARED_USE[stage, n]:
                    pe.wait_ge(shared_drained, SHARED_USE[stage, n])

            def attention(stage, n, i):
                if stage == "scores":
                    r, tiles = SCORES[i]
                    unit = NSC * n + i
                    if i == 0:
                        pe.wait_ge(stack_loaded[n % 2], 16 * (R + 1) * (n // 2 + 1))
                    if unit >= RING:
                        pe.wait_ge(max_done, maxima(unit - RING + 1))
                    for at, t in enumerate(tiles):
                        width = max(P * (t + 1), 2 * P)
                        last = nc.tensor.matmul(ps_scores[:, unit % RING, 2 * P * at:2 * P * at + width],
                                                q_stack[:, n % GROUPS, r, t * P:(t + 1) * P],
                                                k_stack[:, n % GROUPS, 0:width], start=True, stop=True,
                                                skip_group_check=True)
                    last.then_inc(scores_ready, 1)
                elif stage == "max_transpose":
                    shared(stage, n)
                    pe.wait_ge(max_done, NMAX * (n + 1))
                    nc.tensor.transpose(ps_shared[0:R * TILES, 0:P], row_max[:, n % 2], ident[:, :])\
                        .then_inc(shared_filled, 1)
                elif stage == "shifted":
                    j, heads = SHIFTED[i]
                    unit = NSH * n + i
                    if i == 0:
                        pe.wait_ge(max_loaded[n % 2], 16 * (n // 2 + 1))
                    if unit >= RING:
                        pe.wait_ge(exp_done, unit + 1 - RING)
                    nc.tensor.matmul(ps_shifted[:, unit % RING, 0:len(heads) * PT_WIDTH[j]],
                                     k_stack[:, n % GROUPS, j * P:(j + 1) * P],
                                     q_stack[:, n % GROUPS, heads[0]:heads[-1] + 1, P * j:SEQ],
                                     start=True, stop=True).then_inc(shifted_ready, 1)
                elif stage == "pv":
                    j = i
                    pe.wait_ge(causal_done, TILES * n + j + 1)
                    if j == 0:
                        pe.wait_ge(shared_drained, drained("v_project", n // GROUPS))
                        if n:
                            pe.wait_ge(pv_saved, n)
                    for r in range(R):
                        at = PT_AT[j] + r * PT_WIDTH[j]
                        last = nc.tensor.matmul(ps_pv[32 * r:32 * r + 32, j * P:SEQ],
                                                v_ones[:, j, R * (n % GROUPS) + r],
                                                p_t[:, n % 2, at:at + PT_WIDTH[j]],
                                                start=(j == 0), stop=(j == TILES - 1), skip_group_check=True)
                    if j == TILES - 1:
                        last.then_inc(pv_done, 1)
                elif stage == "out_transpose":
                    shared(stage, n)
                    pe.wait_ge(pv_saved, n + 1)
                    for t in range(TILES):
                        last = nc.tensor.transpose(ps_shared[:, t * P:(t + 1) * P],
                                                   pv_s[:, n % 2, t * P:(t + 1) * P], ident[:, :])
                    last.then_inc(shared_filled, 1)
                elif stage in ("x_transpose", "attn_transpose", "x2_transpose"):
                    shared(stage, n)
                    src = {"x_transpose": xn, "attn_transpose": attn, "x2_transpose": x2n}[stage]
                    if stage == "attn_transpose":
                        pe.wait_ge(shared_drained, drained("out_transpose", GROUPS * (n + 1) - 1))
                    else:
                        pe.wait_ge(normalised, TILES * LN_USE["ln1" if stage == "x_transpose" else "ln2", n])
                    for t in range(TILES):
                        last = nc.tensor.transpose(ps_shared[:, t * P:(t + 1) * P], src[:, t], ident[:, :])
                    last.then_inc(shared_filled, 1)
                elif stage in ("q_project", "k_project"):
                    shared(stage, n)
                    if n == 0:
                        pe.wait_ge(w_loaded, 16 * 6)
                    w = qw_s if stage == "q_project" else kw_s
                    nc.tensor.matmul(ps_shared, w[:, :], xn_t[:, n % 2], start=True, stop=True)\
                        .then_inc(shared_filled, 1)
                elif stage == "v_project":
                    shared(stage, n)
                    for t in range(TILES):
                        last = nc.tensor.matmul(ps_shared[:, t * P:(t + 1) * P], xn_t[:, n % 2, t * P:(t + 1) * P],
                                                vw_s[:, :], start=True, stop=True, skip_group_check=True)
                    last.then_inc(shared_filled, 1)
                elif stage == "project":
                    shared(stage, n)
                    for t in range(TILES):
                        last = nc.tensor.matmul(ps_shared[:, t * P:(t + 1) * P], attn_t[:, t * P:(t + 1) * P],
                                                ow_s[:, :], start=True, stop=True, skip_group_check=True)
                    last.then_inc(shared_filled, 1)
                elif stage == "gate":
                    shared(stage, n)
                    for t in range(TILES):
                        last = nc.tensor.matmul(ps_shared[:, t * EXPERTS:(t + 1) * EXPERTS],
                                                x2n_t[:, t * P:(t + 1) * P], wg_s[:, :],
                                                start=True, stop=True, skip_group_check=True)
                    last.then_inc(shared_filled, 1)
                elif stage == "weight_transpose":
                    shared(stage, n)
                    pe.wait_ge(weights_ready, n + 1)
                    nc.tensor.transpose(ps_shared[0:EXPERTS * TILES, 0:P],
                                        weights[:, :, :].rearrange("p e t -> p (e t)"), ident[:, :])\
                        .then_inc(shared_filled, 1)

            def up(local, pair):
                unit = UNITS * 2 * pair + local
                k2, b, f = (local // UNITS) % 2, (local // FT) % BATCHES, local % FT
                if local % UNITS == 0:
                    pe.wait_ge(w12_split, 2 * pair + local // UNITS + 1)
                if peeled(pair, 0) and local < UNITS and f == 0:
                    pe.wait_ge(x2_split, b + 1)
                pe.wait_ge(act_done, 2 * unit + 2)
                cols = slice(f * P, (f + 1) * P)
                for i, (w, xx) in enumerate(((w1_hi, x_hi), (w1_hi, x_lo), (w1_lo, x_hi))):
                    last = nc.tensor.matmul(ps_h[:, f], w[:, k2, cols], xx[:, b], start=(i == 0), stop=(i == 2))
                last.then_inc(h_ready, 1)

            def down(local, pair):
                unit = UNITS * 2 * pair + local
                k2, b, f = local // UNITS, (local // FT) % BATCHES, local % FT
                pe.wait_ge(lo_done, unit + 1)
                if f == 0:
                    pe.wait_ge(y_free, 2 * BATCHES * pair + local // FT + 1)
                for i, (w, aa) in enumerate(((w2_hi, act_hi), (w2_hi, act_lo), (w2_lo, act_hi))):
                    last = nc.tensor.matmul(ps_y[:, (local // FT) % 2], w[:, k2, f], aa[:, f],
                                            start=(f == 0 and i == 0), stop=(f == FT - 1 and i == 2))
                last.then_inc(unit_done, 1)

            def final(b):
                pe.wait_ge(acc_done, 1 + (EXPERTS - 1) * BATCHES + b + 1)
                if b >= 2:
                    pe.wait_ge(out_ready, b - 1)
                for t in range(TILES):
                    last = nc.tensor.transpose(ps_final[:, b % 2, t * P:(t + 1) * P],
                                               acc[:, b, t * P:(t + 1) * P], ident[:, :])
                last.then_inc(final_ready, 1)

            pe.wait_ge(ident_ready, 1)
            for event in MAIN:
                attention(*event)
            pe.sem_inc(unit_done, FT)
            for local in range(-LAG, 2 * UNITS):
                for event in TAIL.get(local, ()):
                    attention(*event)
                if local == -LAG:
                    pe.wait_ge(exp_done, NSH * STEPS)
                if local >= 0:
                    down(local, 0)
                up(local + LAG, 0)
            with pe.Fori(1, LAST_PAIR) as pair:
                for local in range(2 * UNITS):
                    down(local, pair)
                    up(local + LAG, pair)
            for local in range(2 * UNITS):
                down(local, LAST_PAIR)
                if local + LAG < 2 * UNITS:
                    up(local + LAG, LAST_PAIR)
                if local in FINAL_AT:
                    final(FINAL_AT[local])
            final(BATCHES - 1)

        @block.scalar
        def _(act):
            def from_shared(stage, n, dst, src, signal=shared_drained, scale=1.0):
                act.wait_ge(shared_filled, filled(stage, n))
                nc.scalar.activation(dst, src, ACT.Copy, scale=scale).then_inc(signal, 1)

            def from_shared_split(stage, n, full, hi, hi_ready):
                if n:
                    act.wait_ge(qk_lo_ready, 2 * n)
                from_shared(stage, n, full, ps_shared)
                act.wait_ge(shared_drained, drained(stage, n))
                nc.scalar.activation(hi, full, ACT.Copy).then_inc(hi_ready, 1)

            def attention(stage, n, i):
                if stage == "max_transpose":
                    if n >= 2:
                        act.wait_ge(max_loaded[n % 2], 16 * (n // 2))
                    from_shared(stage, n, neg_max[:, n % 2], ps_shared[0:R * TILES, 0:P], scale=-1.0)
                elif stage == "shifted":
                    j, heads = SHIFTED[i]
                    unit = NSH * n + i
                    act.wait_ge(shifted_ready, unit + 1)
                    if i == 0 and n >= 2:
                        act.wait_ge(pv_done, n - 1)
                    at, size = PT_AT[j] + heads[0] * PT_WIDTH[j], len(heads) * PT_WIDTH[j]
                    nc.scalar.activation(p_t[:, n % 2, at:at + size], ps_shifted[:, unit % RING, 0:size],
                                         ACT.Exp, scale=SCALE).then_inc(exp_done, 1)
                elif stage == "pv" and i == TILES - 1:
                    act.wait_ge(pv_done, n + 1)
                    if n >= 2:
                        act.wait_ge(shared_filled, filled("out_transpose", n - 2))
                    nc.scalar.activation(pv_s[:, n % 2], ps_pv, ACT.Copy).then_inc(pv_saved, 1)
                elif stage == "x_transpose":
                    from_shared(stage, n, xn_t[:, n % 2], ps_shared)
                elif stage == "q_project":
                    if n:
                        act.wait_ge(q_written, 16 * 3 * n)
                    from_shared_split(stage, n, qk_f[:, 0], q_hi[:, :], q_hi_ready)
                elif stage == "k_project":
                    if n:
                        act.wait_ge(k_written, 16 * 3 * n)
                    from_shared_split(stage, n, qk_f[:, 1], k_hi[:, :], k_hi_ready)
                elif stage == "v_project":
                    act.wait_ge(v_cleared, 2)
                    from_shared(stage, n, v_ones[:, :, :, 0:HD].rearrange("p t h i -> p t i h"),
                                ps_shared.rearrange("p (t i h) -> p t i h", t=TILES, i=HD))
                elif stage == "attn_transpose":
                    from_shared(stage, n, attn_t[:, :], ps_shared)
                elif stage == "x2_transpose":
                    if n:
                        act.wait_ge(x2_split, n)
                    from_shared(stage, n, x2n_t[:, :], ps_shared)
                elif stage == "weight_transpose":
                    if n:
                        act.wait_ge(weights_written, 16 * n)
                    from_shared(stage, n, weights_t[:, :], ps_shared[0:EXPERTS * TILES, 0:P])

            def activate(local, pair, func):
                unit = UNITS * 2 * pair + local
                slot, f = local // UNITS, local % FT
                if local % UNITS == 0:
                    act.wait_ge(bias_loaded[slot], 16 * 2 * (pair + 1))
                act.wait_ge(h_ready, unit + 1)
                act.wait_ge(unit_done, unit + 1)
                for dst in (act_f, act_hi):
                    nc.scalar.activation(dst[:, f], ps_h[:, f], func, bias=b1_s[:, slot, f:f + 1])\
                        .then_inc(act_done, 1)

            for event in MAIN:
                attention(*event)
            act.sem_inc(act_done, 2 * FT)
            for local in range(2 * UNITS):
                for event in TAIL.get(local - LAG, ()):
                    attention(*event)
                activate(local, 0, ACT.Gelu)
            for func, first, end in ((ACT.Gelu, 1, EXPERTS // 4), (ACT.Silu, EXPERTS // 4, EXPERTS // 2)):
                with act.Fori(first, end) as pair:
                    for local in range(2 * UNITS):
                        activate(local, pair, func)

        @block.vector
        def _(dve):
            chain = [0]

            nc.vector.memset(k_stack[:, GROUPS - 1].bitcast(F32), 1.0).then_inc(ones_ready, 1)

            def mark(ins):
                chain[0] += 1
                ins.then_inc(dve_chain, 1)

            def written():
                dve.wait_ge(dve_chain, chain[0])

            per_expert = lambda s: s.unsqueeze(2).to_broadcast([P, TILES, EXPERTS])
            per_tile = lambda s: s[:, :].unsqueeze(1).to_broadcast([P, TILES, EXPERTS])

            def first_largest(step, values, top, chosen):
                written()
                if step == 0:
                    mark(nc.vector.tensor_reduce(top, values, AX_X, ALU.max))
                elif step == 1:
                    mark(nc.vector.tensor_tensor(equal, values, per_expert(top), ALU.is_equal))
                elif step == 2:
                    mark(nc.vector.tensor_tensor(ranked, equal, per_tile(rank), ALU.mult))
                elif step == 3:
                    mark(nc.vector.tensor_reduce(best, ranked, AX_X, ALU.max))
                elif step == 4:
                    mark(nc.vector.tensor_tensor(chosen, ranked, per_expert(best), ALU.is_equal))

            logits, equal, ranked, first, others, second, part_1, part_2 = (gate_f[:, i] for i in range(8))
            top_1, best, top_2, _, gap, gap_e, total, share_1, share_2 = (gate_s[:, i] for i in range(9))

            def attention(stage, n, i):
                if stage in ("ln1_stats", "ln2_stats"):
                    if i == 0:
                        if stage == "ln2_stats":
                            dve.wait_ge(shared_drained, drained("project", n))
                        else:
                            dve.wait_ge(x_loaded, 16) if n else dve.wait_ge(x0_loaded, 16)
                    if i < TILES:
                        mark(nc.vector.bn_stats(stats[:, i], xs[:, n, i]))
                    else:
                        use = LN_USE[stage[:3], n]
                        if use > 1:
                            dve.wait_ge(normalised, TILES * (use - 1))
                        written()
                        for t in range(TILES):
                            last = nc.vector.bn_aggr(moments[:, t], stats[:, t])
                        mark(last)
                        written()
                        nc.vector.tensor_scalar(var_eps[:, :], moments[:, :, 1], EPS, None, ALU.add)\
                            .then_inc(var_ready, 1)
                elif stage in ("ln1_normalise", "ln2_normalise"):
                    dst, transpose = (xn, "x_transpose") if stage == "ln1_normalise" else (x2n, "x2_transpose")
                    if i == 0:
                        dve.wait_ge(rstd_ready, LN_USE[stage[:3], n])
                        if n:
                            dve.wait_ge(shared_filled, filled(transpose, n - 1))
                    nc.vector.tensor_scalar(dst[:, i], xs[:, n, i], moments[:, i, 0:1], rstd[:, i:i + 1],
                                            ALU.subtract, ALU.mult).then_inc(normalised, 1)
                elif stage == "scores":
                    r, tiles = SCORES[i]
                    unit = NSC * n + i
                    if i == 0:
                        dve.wait_ge(causal_ready, 1)
                        if n >= 2:
                            dve.wait_ge(shared_filled, filled("max_transpose", n - 2))
                    dve.wait_ge(scores_ready, unit + 1)
                    for at, t in enumerate(tiles):
                        count = maxima(unit) + at
                        if count >= 4:
                            dve.wait_ge(max_done, count - 3)
                        width = P * (t + 1)
                        col = r * TILES + t
                        nc.vector.tensor_tensor_reduce(
                            out=scratch[:, count % 4, 0:width],
                            in0=ps_scores[:, unit % RING, 2 * P * at:2 * P * at + width],
                            in1=causal[:, SEQ - width:SEQ], scale=1.0, scalar=MASKED, op0=ALU.add, op1=ALU.max,
                            accum_out=row_max[:, n % 2, col:col + 1]).then_inc(max_done, 1)
                elif stage in ("q_project", "k_project"):
                    side, hi, lo = (0, q_hi, q_lo) if stage == "q_project" else (1, k_hi, k_lo)
                    if n:
                        dve.wait_ge(k_written if side else q_written, 16 * 3 * n)
                    dve.wait_ge(k_hi_ready if side else q_hi_ready, n + 1)
                    nc.vector.tensor_tensor(lo[:, :], qk_f[:, side], hi[:, :].bitcast(F32), ALU.subtract)\
                        .then_inc(qk_lo_ready, 1)
                elif stage == "out_transpose":
                    dve.wait_ge(shared_filled, filled(stage, n))
                    b, g = divmod(n, GROUPS)
                    if g == 0 and b:
                        dve.wait_ge(shared_filled, filled("attn_transpose", b - 1))
                    heads = ps_shared.rearrange("p (t r c) -> p t r c", t=TILES, c=32)
                    mark(nc.vector.reciprocal(rsum[:, :, :], heads[:, :, :, HD]))
                    written()
                    nc.vector.tensor_tensor(
                        attn[:, :, :].rearrange("p t (i g r) -> p t g r i", i=HD, g=GROUPS)[:, :, g],
                        heads[:, :, :, 0:HD], rsum[:, :, :].unsqueeze(3).to_broadcast([P, TILES, R, HD]),
                        ALU.mult).then_inc(shared_drained, 1)
                elif stage == "project":
                    dve.wait_ge(shared_filled, filled(stage, n))
                    flat = xs[:, n].rearrange("p t d -> p (t d)")
                    nc.vector.tensor_tensor(flat, ps_shared, flat, ALU.add).then_inc(shared_drained, 1)
                elif stage == "choose" and i == 0:
                    dve.wait_ge(shared_filled, filled("gate", n))
                    if n:
                        dve.wait_ge(weights_ready, n)
                    else:
                        dve.wait_ge(w_loaded, 16 * 6)
                    nc.vector.tensor_tensor(
                        logits, ps_shared[:, 0:TILES * EXPERTS].rearrange("p (t e) -> p t e", t=TILES),
                        per_tile(bg_s), ALU.add).then_inc(shared_drained, 1)
                elif stage == "choose":
                    if i == 1:
                        dve.wait_ge(shared_drained, drained("gate", n))
                    if 1 <= i < 6:
                        first_largest(i - 1, logits, top_1, first)
                    elif i == 6:
                        written()
                        mark(nc.vector.scalar_tensor_tensor(out=others, in0=first, scalar=MASKED, in1=logits,
                                                            op0=ALU.mult, op1=ALU.add))
                    elif i < 12:
                        first_largest(i - 7, others, top_2, second)
                    else:
                        nc.vector.tensor_tensor(gap, top_2, top_1, ALU.subtract).then_inc(gap_ready, 1)
                elif stage == "share":
                    if i == 0:
                        dve.wait_ge(gap_exp, n + 1)
                        mark(nc.vector.tensor_scalar(total, gap_e, 1.0, None, ALU.add))
                    else:
                        written()
                    if i == 1:
                        mark(nc.vector.reciprocal(share_1, total))
                    elif i == 2:
                        mark(nc.vector.tensor_tensor(share_2, gap_e, share_1, ALU.mult))
                    elif i == 3:
                        nc.vector.tensor_tensor(part_1, first, per_expert(share_1), ALU.mult)
                        mark(nc.vector.tensor_tensor(part_2, second, per_expert(share_2), ALU.mult))
                    elif i == 4:
                        if n:
                            dve.wait_ge(shared_filled, filled("weight_transpose", n - 1))
                        nc.vector.tensor_tensor(weights[:, :, :].rearrange("p e t -> p t e"), part_1, part_2,
                                                ALU.add).then_inc(weights_ready, 1)

            def split_lo(local, pair):
                f = local % FT
                dve.wait_ge(act_done, 2 * (2 * UNITS * pair + local + 1) + 2 * FT)
                nc.vector.tensor_tensor(act_lo[:, f], act_f[:, f], act_hi[:, f].bitcast(F32), ALU.subtract)\
                    .then_inc(lo_done, 1)

            def weigh(q, pair):
                slot, b = q // BATCHES, q % BATCHES
                done = 2 * BATCHES * pair + q
                if q % BATCHES == 0:
                    dve.wait_ge(bias_loaded[slot], 16 * 2 * (pair + 1))
                if peeled(pair, 0) and q in (0, BATCHES - 1):
                    dve.wait_ge(routing_loaded[0], 16 * (BATCHES - 1 if q == 0 else BATCHES))
                elif q % BATCHES == 0:
                    dve.wait_ge(routing_loaded[slot], 16 * BATCHES * (pair + 1))
                dve.wait_ge(unit_done, FT * (done + 1) + FT)
                dve.wait_ge(acc_done, done + 1)
                nc.vector.scalar_tensor_tensor(
                    out=y_w[:, :], in0=ps_y[:, q % 2], scalar=b2_s[:, slot:slot + 1],
                    in1=weight_bc[:, slot, b * SEQ:(b + 1) * SEQ], op0=ALU.add, op1=ALU.mult).then_inc(y_free, 1)

            def accumulate(q, pair):
                b = q % BATCHES
                done = 2 * BATCHES * pair + q
                dve.wait_ge(y_free, done + 1 + 2)
                nc.vector.tensor_tensor(acc[:, b], acc[:, b], y_w[:, :], ALU.add).then_inc(acc_done, 1)

            def expert_unit(local, pair):
                if local + AHEAD_LO < 2 * UNITS or not peeled(pair, LAST_PAIR):
                    split_lo(local + AHEAD_LO, pair)
                if local >= 1 and local % FT == 0:
                    accumulate(local // FT - 1, pair)
                if local >= 0 and local % FT == FT - 1:
                    weigh(local // FT, pair)
                if local == 2 * UNITS - 1:
                    accumulate(2 * BATCHES - 1, pair)

            def add_final(b):
                dve.wait_ge(final_ready, b + 1)
                flat = xs[:, b].rearrange("p t d -> p (t d)")
                nc.vector.tensor_tensor(flat, ps_final[:, b % 2], flat, ALU.add).then_inc(out_ready, 1)

            for event in MAIN:
                attention(*event)
            dve.sem_inc(y_free, 2)
            for local in range(-LAG, 2 * UNITS):
                if local >= -AHEAD_LO:
                    expert_unit(local, 0)
                for event in TAIL.get(local, ()):
                    attention(*event)
            with dve.Fori(1, LAST_PAIR) as pair:
                for local in range(2 * UNITS):
                    expert_unit(local, pair)
            for local in range(2 * UNITS):
                expert_unit(local, LAST_PAIR)
                if local in FINAL_AT:
                    add_final(FINAL_AT[local])
            add_final(BATCHES - 1)

        @block.gpsimd
        def _(pool):
            chain = [0]

            def link(ins):
                chain[0] += 1
                ins.then_inc(pool_chain, 1)
                pool.wait_ge(pool_chain, chain[0])

            link(nc.gpsimd.memset(minus_half[:, :], -0.5))
            link(nc.gpsimd.memset(euler[:, :], math.e))
            link(nc.gpsimd.memset(ident[:, :], 0.0))
            nc.gpsimd.affine_select(out=ident[:, :], in_=ident[:, :], compare_op=ALU.not_equal, fill=1.0, base=0,
                                    pattern=[[-1, P]], channel_multiplier=1).then_inc(ident_ready, 1)
            def clear_operands():
                link(nc.gpsimd.memset(causal[:, :], 0.0))
                tail = causal[:, SEQ - P:SEQ]
                nc.gpsimd.affine_select(out=tail, in_=tail, compare_op=ALU.is_ge, fill=MASKED, base=0,
                                        pattern=[[-1, P]], channel_multiplier=1).then_inc(causal_ready, 1)
                for g in range(1, GROUPS):
                    nc.gpsimd.memset(q_stack[:, g].bitcast(F32), 0.0).then_inc(stacks_cleared, 1)
                nc.gpsimd.memset(v_ones[:, :, :, :], 0.0).then_inc(v_cleared, 1)
                pool.wait_ge(v_cleared, 1)
                nc.gpsimd.memset(v_ones[:, :, :, HD:HD + 1], 1.0).then_inc(v_cleared, 1)
                nc.gpsimd.iota(rank[:, :], [[-1, EXPERTS]], base=EXPERTS, channel_multiplier=0,
                               allow_small_or_imprecise_dtypes=True)
                nc.gpsimd.memset(acc[:, :, :], 0.0).then_inc(acc_done, 1)

            def split(src, hi, lo, signal):
                link(nc.gpsimd.tensor_scalar(hi, src, 1.0, 1.0, ALU.mult, ALU.mult))
                ins = nc.gpsimd.tensor_tensor(lo, src, hi.bitcast(F32), ALU.subtract)
                if signal is not None:
                    ins.then_inc(signal, 1)

            def split_expert(k):
                slot = k % 2
                pool.wait_ge(w12_loaded[slot], 16 * 2 * (k // 2 + 1))
                split(w1_in[:, slot], w1_hi[:, slot], w1_lo[:, slot], None)
                flat = lambda w: w[:, slot].rearrange("p f d -> p (f d)")
                split(flat(w2_in), flat(w2_hi), flat(w2_lo), w12_split)

            nc.gpsimd.memset(q_stack[:, 0].bitcast(F32), 0.0).then_inc(stacks_cleared, 1)
            for stage, n, i in PLAN:
                if stage in ("ln1_power", "ln2_power"):
                    pool.wait_ge(var_ready, LN_USE[stage[:3], n])
                    nc.gpsimd.tensor_tensor(rstd[:, :], var_eps[:, :], minus_half[:, :], ALU.pow)\
                        .then_inc(rstd_ready, 1)
                    if (stage, n) == ("ln1_power", 0):
                        clear_operands()
                elif stage == "shifted":
                    j, heads = SHIFTED[i]
                    if i in LAST_UNIT:
                        pool.wait_ge(exp_done, NSH * n + i + 1)
                        diag = p_t[:, n % 2, PT_AT[j]:PT_AT[j] + R * PT_WIDTH[j]].rearrange(
                            "p (h q) -> p h q", h=R)[:, :, 0:P]
                        nc.gpsimd.affine_select(out=diag, in_=diag, compare_op=ALU.is_ge, fill=0.0, base=0,
                                                pattern=[[0, R], [1, P]], channel_multiplier=-1)\
                            .then_inc(causal_done, 1)
                elif stage == "gap_power":
                    pool.wait_ge(gap_ready, n + 1)
                    nc.gpsimd.tensor_tensor(gate_s[:, 5], euler[:, :], gate_s[:, 4], ALU.pow).then_inc(gap_exp, 1)
                elif stage == "x2_transpose":
                    pool.wait_ge(shared_drained, drained(stage, n))
                    split(x2n_t[:, :], x_hi[:, n], x_lo[:, n], x2_split)
                    if n < 2:
                        split_expert(n)
            for k in range(2, EXPERTS):
                split_expert(k)


def kernel(L0_attn_x, L0_attn_qw, L0_attn_kw, L0_attn_vw, L0_attn_ow,
           L0_ffn_W1, L0_ffn_b1, L0_ffn_W2, L0_ffn_b2, L0_ffn_Wg, L0_ffn_bg):
    import numpy as np
    import concourse.bacc as bacc
    from concourse.bass_utils import run_bass_kernel_spmd

    by_head = lambda w: np.asarray(w).reshape(P, HD, HEADS).transpose(0, 2, 1).reshape(P, P)
    arrays = {
        "x": L0_attn_x, "qw": by_head(L0_attn_qw), "kw": by_head(L0_attn_kw), "vw": L0_attn_vw, "ow": L0_attn_ow,
        "W1": L0_ffn_W1,
        "b1": np.asarray(L0_ffn_b1).reshape(EXPERTS, FT, P).transpose(0, 2, 1),
        "W2": L0_ffn_W2,
        "b2": np.asarray(L0_ffn_b2).reshape(EXPERTS, P, 1),
        "Wg": L0_ffn_Wg, "bg": L0_ffn_bg,
    }
    arrays = {name: np.ascontiguousarray(a) for name, a in arrays.items()}
    nc = bacc.Bacc("TRN2", target_bir_lowering=False, num_devices=1)
    args = [nc.dram_tensor(name, a.shape, F32, kind="ExternalInput").ap() for name, a in arrays.items()]
    out = nc.dram_tensor("out", (BATCHES, SEQ, P), F32, kind="ExternalOutput").ap()
    build(nc, *args, out)
    result = run_bass_kernel_spmd(nc, [arrays], core_ids=[0])
    return result.results[0]["out"]
```
